# Optimizing a Trainium2 kernel written in Bass

```python
import numpy as np
import jax
import jax.numpy as jnp

def _softmax(x, axis=-1):
    return jax.nn.softmax(x, axis=axis)
def _gelu(x):
    return jax.nn.gelu(x, approximate=True)
def _silu(x):
    return jax.nn.silu(x)
def _sigmoid(x):
    return jax.nn.sigmoid(x)
def _layernorm(x, axis=-1, eps=1e-5):
    m = jnp.mean(x, axis=axis, keepdims=True)
    v = jnp.var(x, axis=axis, keepdims=True)
    return (x - m) / jnp.sqrt(v + eps)
def _scatter_add(tgt, idx, src, axis=0):
    return tgt.at[idx].add(src)
def _segment_sum(src, seg, n):
    return jax.ops.segment_sum(src, seg, n)

kernel_name = 'mk_conv_seq_d1_conv_nchw512_fd5e40'

def setup_inputs(seed: int = 0):
    np.random.seed(seed)
    _w = jnp.asarray
    def _rec_inputs():
        import jax
        import jax.numpy as jnp
        _gk = jax.random.key(seed)
        x = -0.0003957 + 1 * jax.random.normal(jax.random.fold_in(_gk, 1), (128, 512, 14, 14), jnp.float32)
        return x
    x = _rec_inputs()
    def _L0_conv_setup():
        import jax, jax.numpy as jnp
        import numpy as np
        B, C, H, W = (128, 512, 14, 14)
        HEADS = 4
        DH = C // HEADS
        RH = RW = 7
        EPS = 1e-05
        SCALE = DH ** (-0.5)

        def _rel_pos_index():
            coords = np.stack(np.meshgrid(np.arange(RH), np.arange(RW), indexing='ij'))
            cf = coords.reshape(2, -1)
            rc = cf[:, :, None] - cf[:, None, :]
            rc = rc.transpose(1, 2, 0).copy()
            rc[:, :, 0] += RH - 1
            rc[:, :, 1] += RW - 1
            rc[:, :, 0] *= 2 * RH - 1
            return rc.sum(-1)
        REL_IDX = _rel_pos_index()

        def batchnorm(x, g, b, m, v):
            inv = g / jnp.sqrt(v + EPS)
            return x * inv[None, :, None, None] + (b - m * inv)[None, :, None, None]

        def dsconv(x, w_dw, w_pw):
            cin = x.shape[1]
            y = jax.lax.conv_general_dilated(x, w_dw, window_strides=(1, 1), padding=((1, 1), (1, 1)), dimension_numbers=('NCHW', 'OIHW', 'NCHW'), feature_group_count=cin)
            return jnp.einsum('bchw,oc->bohw', y, w_pw)

        def bilinear_to_7(x):
            hin, win = (x.shape[2], x.shape[3])
            ys = jnp.linspace(0.0, hin - 1, RH)
            xs = jnp.linspace(0.0, win - 1, RW)
            y0 = jnp.floor(ys).astype(jnp.int32)
            y1 = jnp.minimum(y0 + 1, hin - 1)
            x0 = jnp.floor(xs).astype(jnp.int32)
            x1 = jnp.minimum(x0 + 1, win - 1)
            wy = (ys - y0)[:, None]
            wx = (xs - x0)[None, :]
            v00 = x[:, :, y0][:, :, :, x0]
            v01 = x[:, :, y0][:, :, :, x1]
            v10 = x[:, :, y1][:, :, :, x0]
            v11 = x[:, :, y1][:, :, :, x1]
            top = v00 * (1 - wx) + v01 * wx
            bot = v10 * (1 - wx) + v11 * wx
            return top * (1 - wy) + bot * wy

        def _to_heads(t, h, w):
            b = t.shape[0]
            return jnp.transpose(t.reshape(b, DH, HEADS, h * w), (0, 2, 3, 1))
        key = jax.random.key(seed)
        ks = jax.random.split(key, 16)
        p = {}
        p['x'] = jax.random.normal(ks[0], (B, C, H, W), jnp.float32)
        p['bn1_g'] = jax.random.normal(ks[1], (C,), jnp.float32) * 0.1 + 1.0
        p['bn1_b'] = jax.random.normal(ks[2], (C,), jnp.float32) * 0.1
        p['bn1_m'] = jax.random.normal(ks[3], (C,), jnp.float32) * 0.1
        p['bn1_v'] = jax.random.uniform(ks[4], (C,), jnp.float32, 0.5, 1.5)
        p['w_qkv_dw'] = jax.random.normal(ks[5], (C, 1, 3, 3), jnp.float32) * 0.1
        p['w_qkv_pw'] = jax.random.normal(ks[6], (3 * C, C), jnp.float32) * C ** (-0.5)
        p['rel_table'] = jax.random.normal(ks[7], ((2 * RH - 1) * (2 * RW - 1), HEADS), jnp.float32) * 0.02
        p['w_out_dw'] = jax.random.normal(ks[8], (C, 1, 3, 3), jnp.float32) * 0.1
        p['w_out_pw'] = jax.random.normal(ks[9], (C, C), jnp.float32) * C ** (-0.5)
        p['bn2_g'] = jax.random.normal(ks[10], (C,), jnp.float32) * 0.1 + 1.0
        p['bn2_b'] = jax.random.normal(ks[11], (C,), jnp.float32) * 0.1
        p['bn2_m'] = jax.random.normal(ks[12], (C,), jnp.float32) * 0.1
        p['bn2_v'] = jax.random.uniform(ks[13], (C,), jnp.float32, 0.5, 1.5)
        p['w_mlp'] = jax.random.normal(ks[14], (C, C), jnp.float32) * C ** (-0.5)
        return p
    _L0_conv_all = _L0_conv_setup()
    _L0_conv_in = {k: v for k, v in _L0_conv_all.items() if k in ('bn1_g', 'bn1_b', 'bn1_m', 'bn1_v', 'w_qkv_dw', 'w_qkv_pw', 'rel_table', 'w_out_dw', 'w_out_pw', 'bn2_g', 'bn2_b', 'bn2_m', 'bn2_v', 'w_mlp', )}
    del _L0_conv_all

    return {
        "x": x,
        "L0_conv_bn1_g": _L0_conv_in["bn1_g"],
        "L0_conv_bn1_b": _L0_conv_in["bn1_b"],
        "L0_conv_bn1_m": _L0_conv_in["bn1_m"],
        "L0_conv_bn1_v": _L0_conv_in["bn1_v"],
        "L0_conv_w_qkv_dw": _L0_conv_in["w_qkv_dw"],
        "L0_conv_w_qkv_pw": _L0_conv_in["w_qkv_pw"],
        "L0_conv_rel_table": _L0_conv_in["rel_table"],
        "L0_conv_w_out_dw": _L0_conv_in["w_out_dw"],
        "L0_conv_w_out_pw": _L0_conv_in["w_out_pw"],
        "L0_conv_bn2_g": _L0_conv_in["bn2_g"],
        "L0_conv_bn2_b": _L0_conv_in["bn2_b"],
        "L0_conv_bn2_m": _L0_conv_in["bn2_m"],
        "L0_conv_bn2_v": _L0_conv_in["bn2_v"],
        "L0_conv_w_mlp": _L0_conv_in["w_mlp"],
    }

def reference(x, L0_conv_bn1_g, L0_conv_bn1_b, L0_conv_bn1_m, L0_conv_bn1_v, L0_conv_w_qkv_dw, L0_conv_w_qkv_pw, L0_conv_rel_table, L0_conv_w_out_dw, L0_conv_w_out_pw, L0_conv_bn2_g, L0_conv_bn2_b, L0_conv_bn2_m, L0_conv_bn2_v, L0_conv_w_mlp):
    import jax
    import jax.numpy as jnp
    def _L0_conv_ref(x, bn1_g, bn1_b, bn1_m, bn1_v, w_qkv_dw, w_qkv_pw, rel_table, w_out_dw, w_out_pw, bn2_g, bn2_b, bn2_m, bn2_v, w_mlp):
        import jax, jax.numpy as jnp
        import numpy as np
        B, C, H, W = (128, 512, 14, 14)
        HEADS = 4
        DH = C // HEADS
        RH = RW = 7
        EPS = 1e-05
        SCALE = DH ** (-0.5)

        def _rel_pos_index():
            coords = np.stack(np.meshgrid(np.arange(RH), np.arange(RW), indexing='ij'))
            cf = coords.reshape(2, -1)
            rc = cf[:, :, None] - cf[:, None, :]
            rc = rc.transpose(1, 2, 0).copy()
            rc[:, :, 0] += RH - 1
            rc[:, :, 1] += RW - 1
            rc[:, :, 0] *= 2 * RH - 1
            return rc.sum(-1)
        REL_IDX = _rel_pos_index()

        def batchnorm(x, g, b, m, v):
            inv = g / jnp.sqrt(v + EPS)
            return x * inv[None, :, None, None] + (b - m * inv)[None, :, None, None]

        def dsconv(x, w_dw, w_pw):
            cin = x.shape[1]
            y = jax.lax.conv_general_dilated(x, w_dw, window_strides=(1, 1), padding=((1, 1), (1, 1)), dimension_numbers=('NCHW', 'OIHW', 'NCHW'), feature_group_count=cin)
            return jnp.einsum('bchw,oc->bohw', y, w_pw)

        def bilinear_to_7(x):
            hin, win = (x.shape[2], x.shape[3])
            ys = jnp.linspace(0.0, hin - 1, RH)
            xs = jnp.linspace(0.0, win - 1, RW)
            y0 = jnp.floor(ys).astype(jnp.int32)
            y1 = jnp.minimum(y0 + 1, hin - 1)
            x0 = jnp.floor(xs).astype(jnp.int32)
            x1 = jnp.minimum(x0 + 1, win - 1)
            wy = (ys - y0)[:, None]
            wx = (xs - x0)[None, :]
            v00 = x[:, :, y0][:, :, :, x0]
            v01 = x[:, :, y0][:, :, :, x1]
            v10 = x[:, :, y1][:, :, :, x0]
            v11 = x[:, :, y1][:, :, :, x1]
            top = v00 * (1 - wx) + v01 * wx
            bot = v10 * (1 - wx) + v11 * wx
            return top * (1 - wy) + bot * wy

        def _to_heads(t, h, w):
            b = t.shape[0]
            return jnp.transpose(t.reshape(b, DH, HEADS, h * w), (0, 2, 3, 1))
        out = batchnorm(x, bn1_g, bn1_b, bn1_m, bn1_v)
        qkv = dsconv(out, w_qkv_dw, w_qkv_pw)
        q, k, v = jnp.split(qkv, 3, axis=1)
        k = bilinear_to_7(k)
        v = bilinear_to_7(v)
        q = _to_heads(q, H, W)
        k = _to_heads(k, RH, RW)
        v = _to_heads(v, RH, RW)
        attn = jnp.einsum('bhid,bhjd->bhij', q, k)
        bias = rel_table[REL_IDX.reshape(-1)].reshape(RH, RW, RH * RW, HEADS)
        bias = jnp.repeat(bias, 2, axis=0)
        bias = jnp.repeat(bias, 2, axis=1)
        bias = jnp.transpose(bias.reshape(H * W, RH * RW, HEADS), (2, 0, 1))[None]
        attn = (attn + bias) * SCALE
        attn = jax.nn.softmax(attn, axis=-1)
        o = jnp.einsum('bhij,bhjd->bhid', attn, v)
        o = jnp.transpose(o, (0, 3, 1, 2)).reshape(x.shape[0], C, H, W)
        o = dsconv(o, w_out_dw, w_out_pw)
        out = o + x
        residue = out
        out = batchnorm(out, bn2_g, bn2_b, bn2_m, bn2_v)
        out = jax.nn.relu(out)
        out = jnp.einsum('bchw,oc->bohw', out, w_mlp)
        return out + residue

    def _gn(v, G=32, eps=1e-5):
        B_, C_, H_, W_ = v.shape
        g = v.reshape(B_, G, C_ // G, H_, W_)
        m = jnp.mean(g, axis=(2, 3, 4), keepdims=True)
        s = jnp.var(g, axis=(2, 3, 4), keepdims=True)
        return ((g - m) / jnp.sqrt(s + eps)).reshape(v.shape)

    def _ln_c(v, eps=1e-6):
        m = jnp.mean(v, axis=1, keepdims=True)
        s = jnp.var(v, axis=1, keepdims=True)
        return (v - m) / jnp.sqrt(s + eps)

    def _ln_t(v, eps=1e-5):
        m = jnp.mean(v, axis=-1, keepdims=True)
        s = jnp.var(v, axis=-1, keepdims=True)
        return (v - m) / jnp.sqrt(s + eps)

    def _to_tokens(v):
        B_, C_, H_, W_ = v.shape
        return v.reshape(B_, C_, H_ * W_).transpose(0, 2, 1)
    def _from_tokens(t, like):
        B_, C_, H_, W_ = like.shape
        return t.transpose(0, 2, 1).reshape(B_, C_, H_, W_)

    x = _L0_conv_ref(x, L0_conv_bn1_g, L0_conv_bn1_b, L0_conv_bn1_m, L0_conv_bn1_v, L0_conv_w_qkv_dw, L0_conv_w_qkv_pw, L0_conv_rel_table, L0_conv_w_out_dw, L0_conv_w_out_pw, L0_conv_bn2_g, L0_conv_bn2_b, L0_conv_bn2_m, L0_conv_bn2_v, L0_conv_w_mlp)
    return x


_drawn_inputs = setup_inputs


def setup_inputs(seed=0):
    import zlib

    import numpy as np

    out = dict(_drawn_inputs(seed))
    spreads = {}
    factors = {'L0_conv_bn1_g': 8.0,
     'L0_conv_bn1_b': 8.0,
     'L0_conv_bn1_m': 7.994,
     'L0_conv_bn1_v': 8.0,
     'L0_conv_w_qkv_dw': 4.223,
     'L0_conv_w_qkv_pw': 4.159,
     'L0_conv_rel_table': 200.0,
     'L0_conv_w_out_dw': 4.303,
     'L0_conv_w_out_pw': 4.078,
     'L0_conv_bn2_b': 64.0,
     'L0_conv_bn2_m': 64.0}
    for name, (base, spread) in spreads.items():
        noise = np.random.default_rng([zlib.crc32(name.encode()), seed]).standard_normal(out[name].shape)
        drawn = base * np.exp(spread * noise) if base else spread * noise
        out[name] = jnp.asarray(drawn.astype(out[name].dtype))
    for name, factor in factors.items():
        out[name] = (out[name] * factor).astype(out[name].dtype)
    return out
```

```python
from contextlib import ExitStack

import numpy as np

import concourse.bass as bass
from concourse import mybir

F32 = mybir.dt.float32
F32R = mybir.dt.float32r
ALU = mybir.AluOpType
ACT = mybir.ActivationFunctionType
AX_X = mybir.AxisListType.X

P = 128
B, C, H, W = 128, 512, 14, 14
T = C // P
HEADS, DH = 4, C // 4
HW = H * W
RH = 7
J = RH * RH
JP = 64
EPS = 1e-5
SCALE = DH ** (-0.5)
G = 4
GROUPS = B // G
PITCH = W + 1
IMG = (H + 1) * PITCH
PAD = (G * (H + 1) + 1) * PITCH + 1
ROWS = G * (H + 1) - 1
CONV = ROWS * W
TAPS = [(dy, dx) for dy in range(3) for dx in range(3)]
STEPS = len(TAPS) - 1
PAIR = 2 * HW
GHW = G * HW
HALF = HW // 2


def need(engine, semaphore, count):
    if isinstance(count, int) and count <= 0:
        return
    engine.wait_ge(semaphore, count)


LOOP = dict(OUT0=0, PV0=4, MLP0=8, OUT1A=12, PV1=14, OUT1B=18, MLP1=20, K=24, V=28, Q=30)
FIRST = dict(PV0=0, PV1=4, K=8, V=12, Q=14)
PRE = dict(K=0, V=4, Q=6)
POST = dict(OUT0=0, MLP0=4, OUT1A=8, OUT1B=10, MLP1=12)
PRE_TILES, FIRST_TILES, LOOP_TILES = 14, 22, 38


def base(i):
    if isinstance(i, int) and i == 0:
        return PRE_TILES
    return i * LOOP_TILES + (PRE_TILES + FIRST_TILES - LOOP_TILES)


def tile_no(i, what):
    if isinstance(i, int) and i == -1:
        return PRE[what]
    if isinstance(i, int) and i == 0:
        return base(0) + FIRST[what]
    if isinstance(i, int) and i == GROUPS:
        return base(GROUPS - 1) + LOOP["K"] + POST[what]
    return base(i) + LOOP[what]


def build(nc, x, bn1_g, bn1_b, bn1_m, bn1_v, w_qkv_dw, w_qkv_pw, rel_table, w_out_dw, w_out_pw,
          bn2_g, bn2_b, bn2_m, bn2_v, w_mlp, out):
    with ExitStack() as ctx:
        def sb(name, shape, dt=F32):
            return ctx.enter_context(nc.sbuf_tensor(name, shape, dt))

        def ps(name, shape):
            return ctx.enter_context(nc.psum_tensor(name, shape, F32))

        def sem(name):
            return ctx.enter_context(nc.semaphore(name))

        w_hi = {m: sb(f"w{m}_hi", [P, T, T, P], F32R) for m in ("q", "o", "m")}
        w_lo = {m: sb(f"w{m}_lo", [P, T, T, P], F32R) for m in ("q", "o", "m")}
        w_full = {m: sb(f"w{m}", [P, T, T, P]) for m in ("k", "v")}
        ident = sb("ident", [P, P])
        taps1 = sb("taps1", [P, T, 9])
        taps2 = sb("taps2", [P, T, 9])
        bn_scale = sb("bn_scale", [P, 2, T])
        bn_shift = sb("bn_shift", [P, 2, T])
        bias = sb("bias", [HALF, 2, HEADS, J])
        frac = sb("frac", [P, 2, RH])

        x_in = sb("x_in", [P, 2, G, HW])
        x_pad = sb("x_pad", [P, 2, PAD])
        y_stage = sb("y_stage", [P, 2, CONV])
        y_hi = sb("y_hi", [P, T, GHW], F32R)
        y_lo = sb("y_lo", [P, T, GHW], F32R)
        bil_a = sb("bil_a", [P, G, RH, W])
        bil_b = sb("bil_b", [P, G, RH, W])
        yb = sb("yb", [P, T, G, JP])
        q_sb = sb("q_sb", [P, HEADS, GHW])
        k_sb = sb("k_sb", [P, HEADS, G * J])
        v_sb = sb("v_sb", [P, 2, C])
        s_sb = sb("s_sb", [HALF, 2 * HEADS, 2, JP])
        row_max = sb("row_max", [HALF, 16])
        row_sum = sb("row_sum", [HALF, 16])
        row_inv = sb("row_inv", [HALF, 16])
        pt_sb = sb("pt_sb", [P, HEADS, HW])
        o_pad = sb("o_pad", [P, HEADS, PAD])
        o_hi = sb("o_hi", [P, T, GHW], F32R)
        o_lo = sb("o_lo", [P, T, GHW], F32R)
        res = sb("res", [P, T, PAIR])
        z_sb = sb("z_sb", [P, T, PAIR])
        h_hi = sb("h_hi", [P, T, PAIR], F32R)
        h_lo = sb("h_lo", [P, T, PAIR], F32R)
        bn_in = bil_a[:, 0, 0:4, 0:2 * T].rearrange("p n (k t) -> p n k t", k=2)
        bn_tmp = bil_b[:, 0, 0:3, 0:2 * T].rearrange("p n (k t) -> p n k t", k=2)
        bias_raw = z_sb[0:HALF, 0, :]

        conv_ps = ps("conv_ps", [P, 2, 2 * 512])
        att_ps = ps("att_ps", [P, 2, 512])
        mm_ps = ps("mm_ps", [P, 2, 512])

        params_in = sem("params_in")
        bias_in = sem("bias_in")
        wn_in = [sem(f"wn_in{b}") for b in range(2)]
        ident_zero, ident_done = sem("ident_zero"), sem("ident_done")
        consts_done = sem("consts_done")
        wt_ready, wt_hi, wt_lo = sem("wt_ready"), sem("wt_hi"), sem("wt_lo")
        bn_step, bn_sqrt = sem("bn_step"), sem("bn_sqrt")
        setup_done = sem("setup_done")
        x_ready = [sem(f"x_ready{b}") for b in range(2)]
        res_ready = [sem(f"res_ready{t}") for t in range(T)]
        stored = [sem(f"stored{t}") for t in range(T)]
        bn_done = sem("bn_done")
        fill1, fill2 = sem("fill1"), sem("fill2")
        hi1_done, hi2_done, hih_done = sem("hi1_done"), sem("hi2_done"), sem("hih_done")
        tile_taken = sem("tile_taken")
        exp_done = sem("exp_done")
        pt_taken = sem("pt_taken")
        relu_done = sem("relu_done")
        tap1, tap2 = sem("tap1"), sem("tap2")
        biased, max_done, sum_done, inv_done = sem("biased"), sem("max_done"), sem("sum_done"), sem("inv_done")
        lo1_done, bil_step, bil_done = sem("lo1_done"), sem("bil_step"), sem("bil_done")
        lo2_done, loh_done = sem("lo2_done"), sem("loh_done")
        sub_done, norm_done = sem("sub_done"), sem("norm_done")
        r_done, out_added = sem("r_done"), sem("out_added")
        tile_ready, scores_ready, pt_ready = sem("tile_ready"), sem("scores_ready"), sem("pt_ready")

        x_group = x.rearrange("(g b) (p t) h w -> g t p b (h w)", b=G, t=T)
        x_pair = x.rearrange("(n b) (p t) h w -> n t p b (h w)", b=2, t=T)
        out_pair = out.rearrange("(n b) (p t) h w -> n t p b (h w)", b=2, t=T)
        wn_src = [w_qkv_pw[0:C, :], w_qkv_pw[C:2 * C, :], w_qkv_pw[2 * C:3 * C, :], w_out_pw, w_mlp]
        wn = [q_sb[:, :, :].rearrange("p a b -> p (a b)")[:, 0:T * C].rearrange("p (t c) -> p t c", t=T),
              o_pad[:, :, :].rearrange("p a b -> p (a b)")[:, 0:T * C].rearrange("p (t c) -> p t c", t=T)]
        names = ["q", "k", "v", "o", "m"]

        def inner(pad, b, dy=1, dx=1):
            at = dy * PITCH + dx
            tile = pad[:, b, at:]
            return bass.AP(tile.tensor, tile.offset, [tile.ap[0], [PITCH, ROWS], [1, W]])

        def conv(b):
            return conv_ps[:, b, 0:CONV]

        def conv_rows(b):
            return conv(b).rearrange("p (r c) -> p r c", c=W)

        def staged(b):
            full = y_stage[:, b, :]
            return bass.AP(full.tensor, full.offset, [full.ap[0], [(H + 1) * W, G], [1, HW]])

        def flat(ap):
            return ap.rearrange("p b n -> p (b n)")

        s_rows = s_sb[:, :, :, :].rearrange("p r b j -> p (r b) j")[:, :, 0:J]

        block = ctx.enter_context(nc.Block())

        @block.sync
        def _(sp):
            def load_x(g, t):
                need(sp, bn_done, g * T + (t - 1))
                sp.dma_start(x_in[:, t % 2, :, :], x_group[g, t]).then_inc(x_ready[t % 2], 16)

            def load_res(g, p, t):
                need(sp, stored[t], (g * 2 + p) * 16)
                sp.dma_start(res[:, t, :].rearrange("p (b n) -> p b n", b=2),
                             x_pair[g * 2 + p, t]).then_inc(res_ready[t], 16)

            def store(g, p, t):
                sp.wait_ge(out_added, g * 8 + (4 * p + t + 1))
                sp.dma_start(out_pair[g * 2 + p, t],
                             res[:, t, :].rearrange("p (b n) -> p b n", b=2)).then_inc(stored[t], 16)

            for m in range(2):
                sp.dma_start(wn[m], wn_src[m].rearrange("(p t) c -> p t c", t=T)).then_inc(wn_in[m % 2], 16)
            sp.dma_start(taps1[:, :, :], w_qkv_dw.rearrange("(p t) o a b -> p t (o a b)", t=T)).then_inc(params_in, 16)
            sp.dma_start(taps2[:, :, :], w_out_dw.rearrange("(p t) o a b -> p t (o a b)", t=T)).then_inc(params_in, 16)
            for n, both in enumerate([(bn1_g, bn2_g), (bn1_b, bn2_b), (bn1_m, bn2_m), (bn1_v, bn2_v)]):
                for k, vec in enumerate(both):
                    sp.dma_start(bn_in[:, n, k, :], vec.rearrange("(p t) -> p t", t=T)).then_inc(params_in, 16)
            for t in range(2):
                load_x(0, t)
            for m in range(2, 5):
                sp.wait_ge(wt_ready, 4 * (m - 1))
                sp.dma_start(wn[m % 2], wn_src[m].rearrange("(p t) c -> p t c", t=T)).then_inc(wn_in[m % 2], 16)
            for half in range(2):
                for yy in range(RH):
                    gy = (half * RH + yy) // 2
                    for dup in range(2):
                        src = bass.AP(rel_table.tensor, rel_table.offset + gy * (2 * RH - 1) * HEADS,
                                      [[HEADS, RH], [(2 * RH - 1) * HEADS, RH], [1, RH * HEADS]])
                        at = yy * W + dup
                        dst = bias_raw[at:at + 2 * RH - 1:2, half * J * HEADS:(half + 1) * J * HEADS]
                        sp.dma_start(dst.rearrange("p (a b) -> p a b", a=RH), src).then_inc(bias_in, 16)
            load_x(0, 2)
            load_x(0, 3)
            for t in range(T):
                load_res(0, 0, t)
            load_x(1, 0)
            load_x(1, 1)

            def iteration(i, next_, next2, prev):
                if next_:
                    for t in (2, 3):
                        load_x(i + 1, t)
                if prev:
                    for t in range(T):
                        store(i - 1, 0, t)
                        load_res(i - 1, 1, t)
                if next2:
                    for t in (0, 1):
                        load_x(i + 2, t)
                if prev:
                    for t in range(T):
                        store(i - 1, 1, t)
                        load_res(i, 0, t)

            iteration(0, True, True, False)
            with sp.Fori(1, GROUPS - 2) as i:
                iteration(i, True, True, True)
            iteration(GROUPS - 2, True, False, True)
            iteration(GROUPS - 1, False, False, True)
            for t in range(T):
                store(GROUPS - 1, 0, t)
                load_res(GROUPS - 1, 1, t)
            for t in range(T):
                store(GROUPS - 1, 1, t)
            for t in range(T):
                sp.wait_ge(stored[t], 16 * 2 * GROUPS)

        @block.scalar
        def _(act):
            def norm1(g, t):
                u, b = t // 2, t % 2
                act.wait_ge(x_ready[b], (g * 2 + (u + 1)) * 16)
                need(act, tap1, g * 32 + (16 * u - 1 + b))
                full = x_pad[:, b, PITCH + 1:]
                dst = bass.AP(full.tensor, full.offset, [full.ap[0], [IMG, G], [PITCH, H], [1, W]])
                nc.scalar.activation(dst, x_in[:, b, :, :].rearrange("p b (r c) -> p b r c", c=W), ACT.Identity,
                                     bias=bn_shift[:, 0, t:t + 1], scale=bn_scale[:, 0, t:t + 1]).then_inc(bn_done, 1)

            def first_tap1(g, t):
                u, b = t // 2, t % 2
                if u == 1:
                    act.wait_ge(tap1, g * 32 + (15 + b))
                elif isinstance(g, int) and g == 1:
                    act.wait_ge(tap1, 31 + b)
                elif not (isinstance(g, int) and g == 0):
                    act.wait_ge(tap2, g * 32 + (b - 33))
                act.wait_ge(bn_done, g * T + (t + 1))
                nc.scalar.activation(conv_rows(b), inner(x_pad, b, 0, 0), ACT.Copy,
                                     scale=taps1[:, t, 0:1]).then_inc(fill1, 1)

            def first_tap2(g, t, conv1_between):
                u, b = t // 2, t % 2
                if u == 1:
                    act.wait_ge(tap2, g * 32 + (15 + b))
                elif conv1_between:
                    act.wait_ge(tap1, g * 32 + (63 + b))
                else:
                    act.wait_ge(tap2, g * 32 + (b - 1))
                act.wait_ge(tile_taken, tile_no(g, "PV1") + 4)
                nc.scalar.activation(conv_rows(b), inner(o_pad, t, 0, 0), ACT.Copy,
                                     scale=taps2[:, t, 0:1]).then_inc(fill2, 1)

            def high1(g, t):
                u, b = t // 2, t % 2
                act.wait_ge(tap1, g * 32 + (16 * u + 15 + b))
                if not (isinstance(g, int) and g == 0):
                    act.wait_ge(tile_ready, base(g - 1))
                nc.scalar.activation(y_hi[:, t, :].rearrange("p (b n) -> p b n", b=G), staged(b),
                                     ACT.Copy).then_inc(hi1_done, 1)

            def high2(g, t):
                u, b = t // 2, t % 2
                act.wait_ge(tap2, g * 32 + (16 * u + 15 + b))
                if not (isinstance(g, int) and g == 0):
                    act.wait_ge(tile_ready, tile_no(g, "OUT1B") + 2)
                nc.scalar.activation(o_hi[:, t, :].rearrange("p (b n) -> p b n", b=G), staged(b),
                                     ACT.Copy).then_inc(hi2_done, 1)

            def take(i, what, k, dst, src):
                act.wait_ge(tile_ready, tile_no(i, what) + (k + 1))
                nc.scalar.activation(dst, src, ACT.Copy).then_inc(tile_taken, 1)

            def take_k(i):
                for h in range(HEADS):
                    take(i, "K", h, k_sb[:, h, :], mm_ps[:, h % 2, 0:G * J])

            def take_v(i):
                for p in range(2):
                    take(i, "V", p, v_sb[:, p, :], mm_ps[:, p, :])

            def take_q(i, p, t):
                take(i, "Q", 4 * p + t, q_sb[:, t, PAIR * p:PAIR * (p + 1)], mm_ps[:, t % 2, 0:PAIR])

            def out_tile(p, t):
                return ("OUT0", t) if p == 0 else ("OUT1A", t) if t < 2 else ("OUT1B", t - 2)

            def take_out(i, p, t):
                g = i - 1
                if p == 1:
                    act.wait_ge(out_added, g * 8 + (t + 1))
                what, k = out_tile(p, t)
                take(i, what, k, z_sb[:, t, :], mm_ps[:, t % 2, 0:PAIR])

            def relu(i, p, t):
                g = i - 1
                act.wait_ge(r_done, g * 8 + (4 * p + t + 1))
                nc.scalar.activation(z_sb[:, t, :], res[:, t, :], ACT.Relu, bias=bn_shift[:, 1, t:t + 1],
                                     scale=bn_scale[:, 1, t:t + 1]).then_inc(relu_done, 1)
                act.wait_ge(relu_done, g * 8 + (4 * p + t + 1))
                if p == 1:
                    act.wait_ge(tile_ready, tile_no(i, "MLP0") + 4)
                elif not (isinstance(g, int) and g == 0):
                    act.wait_ge(tile_ready, tile_no(i - 1, "MLP1") + 4)
                nc.scalar.activation(h_hi[:, t, :], z_sb[:, t, :], ACT.Copy).then_inc(hih_done, 1)

            def take_mlp(i, p, t):
                take(i, f"MLP{p}", t, z_sb[:, t, :], mm_ps[:, t % 2, 0:PAIR])

            def exp(i, p):
                act.wait_ge(sub_done, i * 2 + (p + 1))
                nc.scalar.activation(s_rows, s_rows, ACT.Exp, scale=SCALE).then_inc(exp_done, 1)

            def take_pt(i, p):
                act.wait_ge(pt_ready, i * 2 + (p + 1))
                nc.scalar.activation(pt_sb[:, :, :].rearrange("p (a b) n -> p a (b n)", a=2),
                                     att_ps[:, :, 0:PAIR], ACT.Copy).then_inc(pt_taken, 1)

            def take_pv(i, p):
                need(act, tap2, i * 32)
                for hp in range(2):
                    for b in range(2):
                        full = o_pad[:, 2 * hp, PITCH + 1 + IMG * (2 * p + b):]
                        dst = bass.AP(full.tensor, full.offset, [full.ap[0], [PAD, 2], [PITCH, H], [1, W]])
                        take(i, f"PV{p}", 2 * hp + b, dst,
                             mm_ps[:, b, 0:PAIR].rearrange("p (h r c) -> p h r c", h=2, c=W))

            for m, name in enumerate(names):
                for s in range(T):
                    act.wait_ge(wt_ready, 4 * m + s + 1)
                    src = mm_ps[:, s % 2, :].rearrange("p (t n) -> p t n", t=T)
                    if name in w_hi:
                        nc.scalar.activation(w_hi[name][:, s, :, :], src, ACT.Copy).then_inc(wt_hi, 1)
                    else:
                        nc.scalar.activation(w_full[name][:, s, 0:2, :], src[:, 0:2, :], ACT.Copy).then_inc(wt_hi, 1)
            act.wait_ge(bn_step, 1)
            nc.scalar.activation(bn_tmp[:, 1, :, :], bn_tmp[:, 0, :, :], ACT.Sqrt).then_inc(bn_sqrt, 1)
            act.wait_ge(setup_done, 1)
            act.wait_ge(consts_done, 2)

            norm1(0, 0)
            norm1(0, 1)
            first_tap1(0, 0)
            first_tap1(0, 1)
            norm1(0, 2)
            first_tap1(0, 2)
            norm1(0, 3)
            first_tap1(0, 3)
            high1(0, 0)
            high1(0, 1)
            norm1(1, 0)
            norm1(1, 1)
            first_tap1(1, 0)
            first_tap1(1, 1)
            high1(0, 2)
            high1(0, 3)
            take_k(-1)
            take_v(-1)
            for p in range(2):
                for t in range(T):
                    take_q(-1, p, t)

            def iteration(i, next_, next2, prev):
                g = i + 1
                if prev:
                    high2(i - 1, 2)
                    high2(i - 1, 3)
                exp(i, 0)
                if prev:
                    take_out(i, 0, 0)
                    take_out(i, 0, 1)
                    relu(i, 0, 0)
                    take_out(i, 0, 2)
                    relu(i, 0, 1)
                    take_out(i, 0, 3)
                    relu(i, 0, 2)
                    relu(i, 0, 3)
                take_pt(i, 0)
                take_pv(i, 0)
                if next_:
                    for t in (2, 3):
                        norm1(g, t)
                        first_tap1(g, t)
                exp(i, 1)
                if next_:
                    high1(g, 0)
                    high1(g, 1)
                if prev:
                    for t in range(T):
                        take_mlp(i, 0, t)
                    take_out(i, 1, 0)
                    take_out(i, 1, 1)
                    relu(i, 1, 0)
                    relu(i, 1, 1)
                take_pt(i, 1)
                take_pv(i, 1)
                if prev:
                    take_out(i, 1, 2)
                    take_out(i, 1, 3)
                    relu(i, 1, 2)
                    relu(i, 1, 3)
                for t in (0, 1):
                    first_tap2(i, t, next_)
                if next_:
                    high1(g, 2)
                    high1(g, 3)
                if next2:
                    norm1(g + 1, 0)
                    norm1(g + 1, 1)
                if prev:
                    for t in range(T):
                        take_mlp(i, 1, t)
                if next_:
                    take_k(i)
                    take_v(i)
                for t in (2, 3):
                    first_tap2(i, t, next_)
                high2(i, 0)
                high2(i, 1)
                if next_:
                    for p in range(2):
                        for t in range(T):
                            take_q(i, p, t)
                if next2:
                    first_tap1(g + 1, 0)
                    first_tap1(g + 1, 1)

            iteration(0, True, True, False)
            with act.Fori(1, GROUPS - 2) as i:
                iteration(i, True, True, True)
            iteration(GROUPS - 2, True, False, True)
            iteration(GROUPS - 1, False, False, True)
            i = GROUPS
            high2(i - 1, 2)
            high2(i - 1, 3)
            for p in range(2):
                for t in range(T):
                    take_out(i, p, t)
                    relu(i, p, t)
                for t in range(T):
                    take_mlp(i, p, t)

        @block.vector
        def _(dve):
            def conv_unit(taps, source, tap_done, filled, g, u, stage_free, between):
                for k in range(2 * STEPS):
                    if k in between:
                        between[k]()
                    b, step = k % 2, k // 2 + 1
                    t = 2 * u + b
                    dy, dx = TAPS[step]
                    if step == 1:
                        dve.wait_ge(filled, g * T + (t + 1))
                    else:
                        dve.wait_ge(tap_done, g * 32 + (16 * u + k - 1))
                    dst = conv(b).rearrange("p (r c) -> p r c", c=W)
                    if step == STEPS:
                        stage_free(b)
                        dst = y_stage[:, b, :].rearrange("p (r c) -> p r c", c=W)
                    nc.vector.scalar_tensor_tensor(
                        out=dst, in0=inner(source, t if source is o_pad else b, dy, dx),
                        scalar=taps[:, t, 3 * dy + dx:3 * dy + dx + 1],
                        in1=conv_rows(b), op0=ALU.mult, op1=ALU.add).then_inc(tap_done, 1)

            def conv1(g, u, between):
                def stage_free(b):
                    if u == 1:
                        dve.wait_ge(bil_done, g * T + (b + 1))
                    elif isinstance(g, int) and g == 1:
                        dve.wait_ge(bil_done, 3 + b)
                    elif not (isinstance(g, int) and g == 0):
                        dve.wait_ge(lo2_done, g * T + (b - 5))
                conv_unit(taps1, x_pad, tap1, fill1, g, u, stage_free, between)

            def conv2(g, u, conv1_between):
                def stage_free(b):
                    if u == 1:
                        dve.wait_ge(lo2_done, g * T + (b + 1))
                    elif conv1_between:
                        dve.wait_ge(bil_done, g * T + (7 + b))
                    else:
                        dve.wait_ge(lo2_done, g * T + (b - 1))
                conv_unit(taps2, o_pad, tap2, fill2, g, u, stage_free, {})

            def bias_max(i, p):
                for b in range(2):
                    dve.wait_ge(scores_ready, i * 4 + (2 * p + b + 1))
                    if b == 0:
                        need(dve, pt_ready, i * 2 + p)
                    nc.vector.tensor_tensor(s_sb[:, :, b, 0:J], att_ps[0:HALF, b, 0:PAIR].rearrange("p (r j) -> p r j", j=J),
                                            bias[:, :, :, :].rearrange("p a h j -> p (a h) j"),
                                            ALU.add).then_inc(biased, 1)
                dve.wait_ge(biased, i * 4 + (2 * p + 2))
                nc.vector.tensor_reduce(row_max[:, :], s_rows, AX_X, ALU.max).then_inc(max_done, 1)

            def sum_inv(i, p):
                dve.wait_ge(exp_done, i * 2 + (p + 1))
                nc.vector.tensor_reduce(row_sum[:, :], s_rows, AX_X, ALU.add).then_inc(sum_done, 1)
                dve.wait_ge(sum_done, i * 2 + (p + 1))
                nc.vector.reciprocal(row_inv[:, :], row_sum[:, :]).then_inc(inv_done, 1)

            nc.vector.memset(x_pad[:, :, :], 0.0)
            nc.vector.memset(yb[:, :, :, :], 0.0)
            nc.vector.memset(s_sb[:, :, :, :], 0.0).then_inc(consts_done, 1)
            gamma, beta, mean, var = (bn_in[:, n, :, :] for n in range(4))
            a, root, t3 = (bn_tmp[:, n, :, :] for n in range(3))
            dve.wait_ge(params_in, 16 * 10)
            steps = [0]

            def step(instruction):
                steps[0] += 1
                instruction.then_inc(bn_step, 1)
                dve.wait_ge(bn_step, steps[0])

            step(nc.vector.tensor_scalar(a, var, EPS, None, ALU.add))
            for m, name in enumerate(names):
                for s in range(T):
                    dve.wait_ge(wt_ready, 4 * m + s + 1)
                    dve.wait_ge(wt_hi, 4 * m + s + 1)
                    src = mm_ps[:, s % 2, :].rearrange("p (t n) -> p t n", t=T)
                    if name in w_hi:
                        nc.vector.tensor_tensor(w_lo[name][:, s, :, :], src, w_hi[name][:, s, :, :].bitcast(F32),
                                                ALU.subtract).then_inc(wt_lo, 1)
                    else:
                        nc.vector.tensor_copy(w_full[name][:, s, 2:4, :], src[:, 2:4, :]).then_inc(wt_lo, 1)
            nc.vector.memset(o_pad[:, :, :], 0.0)
            dve.wait_ge(bn_sqrt, 1)
            step(nc.vector.reciprocal(t3, root))
            step(nc.vector.tensor_tensor(t3, t3, a, ALU.mult))
            step(nc.vector.tensor_tensor(t3, t3, root, ALU.add))
            step(nc.vector.tensor_scalar(t3, t3, 0.5, None, ALU.mult))
            step(nc.vector.reciprocal(root, t3))
            step(nc.vector.tensor_tensor(bn_scale[:, :, :], root, gamma, ALU.mult))
            step(nc.vector.tensor_tensor(t3, bn_scale[:, :, :], mean, ALU.mult))
            step(nc.vector.tensor_tensor(bn_shift[:, :, :], beta, t3, ALU.subtract))
            dve.wait_ge(bias_in, 16 * 4 * RH)
            for half in range(2):
                raw = bias_raw[:, half * J * HEADS:(half + 1) * J * HEADS]
                backwards = bass.AP(raw.tensor, raw.offset + (J - 1) * HEADS, [raw.ap[0], [1, HEADS], [-HEADS, J]])
                last = nc.vector.tensor_copy(bias[:, half, :, :], backwards)
            step(last)
            nc.vector.memset(row_inv[:, :], 0.0).then_inc(setup_done, 1)

            conv1(0, 0, {})
            conv1(0, 1, {})

            def iteration(i, next_, next2, prev):
                if next_:
                    conv1(i + 1, 0, {0: lambda: bias_max(i, 0), 6: lambda: sum_inv(i, 0),
                                     15: lambda: bias_max(i, 1)})
                    conv1(i + 1, 1, {6: lambda: sum_inv(i, 1)})
                else:
                    for p in range(2):
                        bias_max(i, p)
                        sum_inv(i, p)
                conv2(i, 0, next_)
                conv2(i, 1, next_)

            iteration(0, True, True, False)
            with dve.Fori(1, GROUPS - 2) as i:
                iteration(i, True, True, True)
            iteration(GROUPS - 2, True, False, True)
            iteration(GROUPS - 1, False, False, True)

        @block.gpsimd
        def _(pool):
            def low1(g, t):
                b = t % 2
                pool.wait_ge(hi1_done, g * T + (t + 1))
                nc.gpsimd.tensor_tensor(y_lo[:, t, :].rearrange("p (b n) -> p b n", b=G), staged(b),
                                        y_hi[:, t, :].bitcast(F32).rearrange("p (b n) -> p b n", b=G),
                                        ALU.subtract).then_inc(lo1_done, 1)
                full = y_stage[:, b, :]

                def rows(odd):
                    return bass.AP(full.tensor, full.offset + odd * W,
                                   [full.ap[0], [(H + 1) * W, G], [2 * W, RH], [1, W]])

                def by_row(w):
                    f = frac[:, w, :]
                    return bass.AP(f.tensor, f.offset, [f.ap[0], [0, G], [1, RH], [0, W]])

                def by_column(w):
                    f = frac[:, w, :]
                    return bass.AP(f.tensor, f.offset, [f.ap[0], [0, G * RH], [1, RH]])

                columns = bil_a[:, :, :, :].rearrange("p b r c -> p (b r) c")
                left = bil_b[:, 0:2, :, :].rearrange("p b r c -> p (b r c)").rearrange("p (r c) -> p r c", c=RH)
                right = bil_b[:, 2:4, :, :].rearrange("p b r c -> p (b r c)").rearrange("p (r c) -> p r c", c=RH)
                n = g * 20 + 5 * t
                need(pool, bil_done, g * T + t)
                nc.gpsimd.tensor_tensor(bil_a[:, :, :, :], rows(0), by_row(0), ALU.mult).then_inc(bil_step, 1)
                nc.gpsimd.tensor_tensor(bil_b[:, :, :, :], rows(1), by_row(1), ALU.mult).then_inc(bil_step, 1)
                pool.wait_ge(bil_step, n + 2)
                nc.gpsimd.tensor_tensor(bil_a[:, :, :, :], bil_a[:, :, :, :], bil_b[:, :, :, :],
                                        ALU.add).then_inc(bil_step, 1)
                pool.wait_ge(bil_step, n + 3)
                nc.gpsimd.tensor_tensor(left, columns[:, :, 0:W:2], by_column(0), ALU.mult).then_inc(bil_step, 1)
                nc.gpsimd.tensor_tensor(right, columns[:, :, 1:W:2], by_column(1), ALU.mult).then_inc(bil_step, 1)
                pool.wait_ge(bil_step, n + 5)
                nc.gpsimd.tensor_tensor(yb[:, t, :, 0:J], left.rearrange("p (b r) c -> p b (r c)", b=G),
                                        right.rearrange("p (b r) c -> p b (r c)", b=G), ALU.add).then_inc(bil_done, 1)

            def low2(g, t):
                pool.wait_ge(hi2_done, g * T + (t + 1))
                nc.gpsimd.tensor_tensor(o_lo[:, t, :].rearrange("p (b n) -> p b n", b=G), staged(t % 2),
                                        o_hi[:, t, :].bitcast(F32).rearrange("p (b n) -> p b n", b=G),
                                        ALU.subtract).then_inc(lo2_done, 1)

            def wide(row):
                return bass.AP(row[:, :].tensor, row[:, :].offset, [row[:, :].ap[0], [1, 16], [0, J]])

            def less_max(i, p):
                pool.wait_ge(max_done, i * 2 + (p + 1))
                nc.gpsimd.tensor_tensor(s_rows, s_rows, wide(row_max), ALU.subtract).then_inc(sub_done, 1)

            def normalise(i, p):
                pool.wait_ge(inv_done, i * 2 + (p + 1))
                nc.gpsimd.tensor_tensor(s_rows, s_rows, wide(row_inv), ALU.mult).then_inc(norm_done, 1)

            def out_tile(p, t):
                return ("OUT0", t) if p == 0 else ("OUT1A", t) if t < 2 else ("OUT1B", t - 2)

            def residual(i, p, t):
                g = i - 1
                pool.wait_ge(res_ready[t], (g * 2 + (p + 1)) * 16)
                what, k = out_tile(p, t)
                pool.wait_ge(tile_taken, tile_no(i, what) + (k + 1))
                nc.gpsimd.tensor_tensor(res[:, t, :], z_sb[:, t, :], res[:, t, :], ALU.add).then_inc(r_done, 1)

            def lowh(i, p, t):
                g = i - 1
                pool.wait_ge(hih_done, g * 8 + (4 * p + t + 1))
                nc.gpsimd.tensor_tensor(h_lo[:, t, :], z_sb[:, t, :], h_hi[:, t, :].bitcast(F32),
                                        ALU.subtract).then_inc(loh_done, 1)

            def add_mlp(i, p, t):
                pool.wait_ge(tile_taken, tile_no(i, f"MLP{p}") + (t + 1))
                nc.gpsimd.tensor_tensor(res[:, t, :], z_sb[:, t, :], res[:, t, :], ALU.add).then_inc(out_added, 1)

            nc.gpsimd.memset(ident[:, :], 0.0).then_inc(ident_zero, 1)
            pool.wait_ge(ident_zero, 1)
            nc.gpsimd.affine_select(out=ident[:, :], in_=ident[:, :], compare_op=ALU.not_equal, fill=1.0, base=0,
                                    pattern=[[-1, P]], channel_multiplier=1).then_inc(ident_done, 1)
            at = np.linspace(0.0, H - 1, RH, dtype=np.float32)
            for j in range(RH):
                w = float(np.float32(at[j] - np.float32(2 * j)))
                nc.gpsimd.memset(frac[:, 0, j:j + 1], float(np.float32(1.0) - np.float32(w)))
                last = nc.gpsimd.memset(frac[:, 1, j:j + 1], w)
            last.then_inc(consts_done, 1)
            pool.wait_ge(consts_done, 2)
            for t in range(T):
                low1(0, t)

            def iteration(i, next_, next2, prev):
                g = i + 1
                if prev:
                    low2(i - 1, 2)
                    low2(i - 1, 3)
                less_max(i, 0)
                if prev:
                    residual(i, 0, 0)
                    residual(i, 0, 1)
                    lowh(i, 0, 0)
                    residual(i, 0, 2)
                    lowh(i, 0, 1)
                normalise(i, 0)
                if prev:
                    residual(i, 0, 3)
                    lowh(i, 0, 2)
                    lowh(i, 0, 3)
                less_max(i, 1)
                if next_:
                    low1(g, 0)
                if prev:
                    for t in range(3):
                        add_mlp(i, 0, t)
                normalise(i, 1)
                if prev:
                    add_mlp(i, 0, 3)
                    residual(i, 1, 0)
                    residual(i, 1, 1)
                    lowh(i, 1, 0)
                    lowh(i, 1, 1)
                if next_:
                    low1(g, 1)
                if prev:
                    residual(i, 1, 2)
                    residual(i, 1, 3)
                    lowh(i, 1, 2)
                    lowh(i, 1, 3)
                if next_:
                    low1(g, 2)
                    low1(g, 3)
                if prev:
                    for t in range(T):
                        add_mlp(i, 1, t)
                low2(i, 0)
                low2(i, 1)

            iteration(0, True, True, False)
            with pool.Fori(1, GROUPS - 2) as i:
                iteration(i, True, True, True)
            iteration(GROUPS - 2, True, False, True)
            iteration(GROUPS - 1, False, False, True)
            i = GROUPS
            low2(i - 1, 2)
            low2(i - 1, 3)
            for p in range(2):
                for t in range(T):
                    residual(i, p, t)
                    lowh(i, p, t)
                for t in range(T):
                    add_mlp(i, p, t)

        @block.tensor
        def _(pe):
            def product(n, k, name, hi, lo, s_ready, p, t, cols):
                need(pe, tile_taken, n + (k - 1))
                dst = mm_ps[:, k % 2, 0:PAIR]
                for s in range(T):
                    s_ready(s)
                    sides = [(w_hi, hi), (w_hi, lo), (w_lo, hi)]
                    for m, (w, r) in enumerate(sides):
                        last = nc.tensor.matmul(dst, w[name][:, s, t, :], r[:, s, cols:cols + PAIR],
                                                start=(s == 0 and m == 0), stop=(s == T - 1 and m == 2))
                last.then_inc(tile_ready, 1)

            def out_product(i, p, t):
                g = i - 1
                what, k = ("OUT0", t) if p == 0 else ("OUT1A", t) if t < 2 else ("OUT1B", t - 2)

                def s_ready(s):
                    if p == 0 and t == 0:
                        pe.wait_ge(lo2_done, g * T + (s + 1))
                product(tile_no(i, what), k, "o", o_hi, o_lo, s_ready, p, t, PAIR * p)

            def mlp(i, p):
                g = i - 1
                for t in range(T):
                    def s_ready(s):
                        if t == 0:
                            pe.wait_ge(loh_done, g * 8 + (4 * p + s + 1))
                    product(tile_no(i, f"MLP{p}"), t, "m", h_hi, h_lo, s_ready, p, t, 0)

            def queries(i, g):
                for p in range(2):
                    for t in range(T):
                        def s_ready(s):
                            if p == 0 and t == 0:
                                pe.wait_ge(lo1_done, g * T + (s + 1))
                        product(tile_no(i, "Q"), 4 * p + t, "q", y_hi, y_lo, s_ready, p, t, PAIR * p)

            def keys(i, g):
                n = tile_no(i, "K")
                for h in range(HEADS):
                    need(pe, tile_taken, n + (h - 1))
                    for s in range(T):
                        if h == 0:
                            pe.wait_ge(bil_done, g * T + (s + 1))
                        last = nc.tensor.matmul(mm_ps[:, h % 2, 0:G * J], w_full["k"][:, s, h, :],
                                                yb[:, s, :, 0:J], start=(s == 0), stop=(s == T - 1))
                    last.then_inc(tile_ready, 1)

            def values(i):
                n = tile_no(i, "V")
                for p in range(2):
                    pe.wait_ge(tile_taken, n + (p - 1))
                    for s in range(T):
                        last = nc.tensor.matmul(mm_ps[:, p, :], yb[:, s, 2 * p:2 * p + 2, :].rearrange("p b j -> p (b j)"),
                                                w_full["v"][:, s, :, :].rearrange("p t n -> p (t n)"),
                                                start=(s == 0), stop=(s == T - 1))
                    last.then_inc(tile_ready, 1)

            def scores(i, p):
                if p == 0:
                    pe.wait_ge(tile_taken, base(i))
                need(pe, pt_taken, i * 2 + p)
                for b in range(2):
                    for half in range(2):
                        for h in range(HEADS):
                            at = PAIR * p + HW * b + HALF * half
                            to = (half * HEADS + h) * J
                            last = nc.tensor.matmul(att_ps[0:HALF, b, to:to + J], q_sb[:, h, at:at + HALF],
                                                    k_sb[:, h, J * (2 * p + b):J * (2 * p + b + 1)],
                                                    start=True, stop=True)
                    last.then_inc(scores_ready, 1)

            def attend(i, p):
                pe.wait_ge(norm_done, i * 2 + (p + 1))
                for half in range(2):
                    for h in range(HEADS):
                        both = s_sb[:, half * HEADS + h, :, :].rearrange("p b j -> p (b j)")
                        at = HW * (h % 2) + HALF * half
                        last = nc.tensor.transpose(att_ps[:, h // 2, at:at + HALF], both, ident[0:HALF, 0:HALF])
                last.then_inc(pt_ready, 1)
                pe.wait_ge(pt_taken, i * 2 + (p + 1))
                n = tile_no(i, f"PV{p}")
                for h in range(HEADS):
                    for b in range(2):
                        if h % 2 == 0:
                            pe.wait_ge(tile_taken, n + (h + b - 1))
                        mm = nc.tensor.matmul(mm_ps[:, b, HW * (h % 2):HW * (h % 2 + 1)],
                                              v_sb[JP * b:JP * b + J, p, DH * h:DH * (h + 1)],
                                              pt_sb[JP * b:JP * b + J, h, :], start=True, stop=True)
                        if h % 2:
                            mm.then_inc(tile_ready, 1)

            pe.wait_ge(ident_done, 1)
            for m in range(5):
                pe.wait_ge(wn_in[m % 2], 16 * (m // 2 + 1))
                for s in range(T):
                    n = 4 * m + s
                    need(pe, wt_hi, n - 1)
                    need(pe, wt_lo, n - 1)
                    for t in range(T):
                        last = nc.tensor.transpose(mm_ps[:, s % 2, P * t:P * (t + 1)], wn[m % 2][:, t, s:C:T],
                                                   ident[:, :])
                    last.then_inc(wt_ready, 1)
            pe.wait_ge(wt_hi, 20)
            pe.wait_ge(wt_lo, 20)
            keys(-1, 0)
            values(-1)
            queries(-1, 0)

            def iteration(i, next_, next2, prev):
                scores(i, 0)
                if prev:
                    for t in range(T):
                        out_product(i, 0, t)
                attend(i, 0)
                scores(i, 1)
                if prev:
                    mlp(i, 0)
                    out_product(i, 1, 0)
                    out_product(i, 1, 1)
                attend(i, 1)
                if prev:
                    out_product(i, 1, 2)
                    out_product(i, 1, 3)
                    mlp(i, 1)
                if next_:
                    keys(i, i + 1)
                    values(i)
                    queries(i, i + 1)

            iteration(0, True, True, False)
            with pe.Fori(1, GROUPS - 2) as i:
                iteration(i, True, True, True)
            iteration(GROUPS - 2, True, False, True)
            iteration(GROUPS - 1, False, False, True)
            i = GROUPS
            for p in range(2):
                for t in range(T):
                    out_product(i, p, t)
                mlp(i, p)


_INS = ['x', 'L0_conv_bn1_g', 'L0_conv_bn1_b', 'L0_conv_bn1_m', 'L0_conv_bn1_v', 'L0_conv_w_qkv_dw',
        'L0_conv_w_qkv_pw', 'L0_conv_rel_table', 'L0_conv_w_out_dw', 'L0_conv_w_out_pw', 'L0_conv_bn2_g',
        'L0_conv_bn2_b', 'L0_conv_bn2_m', 'L0_conv_bn2_v', 'L0_conv_w_mlp']
_OUTS = [((B, C, H, W), 'float32')]


def kernel(**inputs):
    import numpy as _np
    import concourse.bacc as _bacc
    from concourse import mybir as _mybir
    from concourse.bass_utils import run_bass_kernel_spmd as _run

    nc = _bacc.Bacc("TRN2", target_bir_lowering=False, num_devices=1)
    arrays, args = {}, []
    for name in _INS:
        a = _np.ascontiguousarray(inputs[name])
        arrays[f"in_{name}_dram"] = a
        args.append(nc.dram_tensor(f"in_{name}_dram", a.shape, _mybir.dt.from_np(a.dtype), kind="ExternalInput").ap())
    for i, (shape, dtype) in enumerate(_OUTS):
        dt = _mybir.dt.from_np(_np.dtype(dtype))
        args.append(nc.dram_tensor(f"out_{i}_dram", shape, dt, kind="ExternalOutput").ap())
    build(nc, *args)
    r = _run(nc, [arrays], core_ids=[0])
    got = tuple(r.results[0][f"out_{i}_dram"] for i in range(len(_OUTS)))
    return got[0]
```

```python
from contextlib import ExitStack

import numpy as np

import concourse.bass as bass
from concourse import mybir

F32 = mybir.dt.float32
F32R = mybir.dt.float32r
ALU = mybir.AluOpType
ACT = mybir.ActivationFunctionType
AX_X = mybir.AxisListType.X

P = 128
B, C, H, W = 128, 512, 14, 14
T = C // P
HEADS, DH = 4, C // 4
HW = H * W
RH = 7
J = RH * RH
JP = 64
EPS = 1e-5
SCALE = DH ** (-0.5)
G = 4
GROUPS = B // G
PITCH = W + 1
IMG = (H + 1) * PITCH
PAD = (G * (H + 1) + 1) * PITCH + 1
ROWS = G * (H + 1) - 1
CONV = ROWS * W
TAPS = [(dy, dx) for dy in range(3) for dx in range(3)]
STEPS = len(TAPS) - 1
PAIR = 2 * HW
GHW = G * HW
HALF = HW // 2


def need(engine, semaphore, count):
    if isinstance(count, int) and count <= 0:
        return
    engine.wait_ge(semaphore, count)


LOOP = dict(OUT1B=0, Q0=2, K=6, V=10, MLP1=12, Q1=16, PV0=20, OUT0=24, OUT1A=28, PV1=30, END=34)
ITER = {0: dict(Q0=0, K=4, V=8, Q1=10, PV0=14, PV1=18, END=22),
        1: dict(Q0=22, K=26, V=30, Q1=32, PV0=36, OUT0=40, OUT1A=44, PV1=46, END=50)}
SHIFT = ITER[1]["END"] - 2 * LOOP["END"]
LAST = GROUPS * LOOP["END"] + SHIFT
ITER[GROUPS] = dict(OUT1B=LAST, MLP1=LAST + 2, OUT0=LAST + 6, OUT1A=LAST + 10, END=LAST + 12)
ITER[GROUPS + 1] = dict(OUT1B=LAST + 12, MLP1=LAST + 14, END=LAST + 18)


def tile_no(i, what):
    if isinstance(i, int) and i in ITER:
        return ITER[i][what]
    return i * LOOP["END"] + (LOOP[what] + SHIFT)


def out_tile(g, p, t):
    if p == 0:
        return tile_no(g + 1, "OUT0") + t
    return tile_no(g + 1, "OUT1A") + t if t < 2 else tile_no(g + 2, "OUT1B") + (t - 2)


def works(i):
    if not isinstance(i, int):
        return True, True, True, True, True
    return 1 <= i <= GROUPS, i < GROUPS, i < GROUPS - 1, 1 <= i <= GROUPS, i >= 2


def build(nc, x, bn1_g, bn1_b, bn1_m, bn1_v, w_qkv_dw, w_qkv_pw, rel_table, w_out_dw, w_out_pw,
          bn2_g, bn2_b, bn2_m, bn2_v, w_mlp, out):
    with ExitStack() as ctx:
        def sb(name, shape, dt=F32):
            return ctx.enter_context(nc.sbuf_tensor(name, shape, dt))

        def ps(name, shape):
            return ctx.enter_context(nc.psum_tensor(name, shape, F32))

        def sem(name):
            return ctx.enter_context(nc.semaphore(name))

        w_hi = {m: sb(f"w{m}_hi", [P, T, T, P], F32R) for m in ("q", "o", "m")}
        w_lo = {m: sb(f"w{m}_lo", [P, T, T, P], F32R) for m in ("q", "o", "m")}
        w_full = {m: sb(f"w{m}", [P, T, T, P]) for m in ("k", "v")}
        ident = sb("ident", [P, P])
        taps1 = sb("taps1", [P, T, 9])
        taps2 = sb("taps2", [P, T, 9])
        bn_scale = sb("bn_scale", [P, 2, T])
        bn_shift = sb("bn_shift", [P, 2, T])
        bias = sb("bias", [HALF, 2, HEADS, J])
        frac = sb("frac", [P, 2, RH])

        x_in = sb("x_in", [P, 2, G, HW])
        x_pad = sb("x_pad", [P, 2, PAD])
        y_stage = sb("y_stage", [P, 2, CONV])
        y_hi = sb("y_hi", [P, T, GHW], F32R)
        y_lo = sb("y_lo", [P, T, GHW], F32R)
        bil_a = sb("bil_a", [P, G, RH, W])
        bil_b = sb("bil_b", [P, G, RH, W])
        yb = sb("yb", [P, T, G, JP])
        q_sb = sb("q_sb", [P, HEADS, GHW])
        k_sb = sb("k_sb", [P, HEADS, G * J])
        v_sb = sb("v_sb", [P, 2, C])
        s_sb = sb("s_sb", [HALF, 2 * HEADS, 2, JP])
        row_max = sb("row_max", [HALF, 16])
        row_sum = sb("row_sum", [HALF, 16])
        row_inv = sb("row_inv", [HALF, 16])
        pt_sb = sb("pt_sb", [P, HEADS, HW])
        o_pad = sb("o_pad", [P, HEADS, PAD])
        o_hi = sb("o_hi", [P, T, GHW], F32R)
        o_lo = sb("o_lo", [P, T, GHW], F32R)
        res = sb("res", [P, T, PAIR])
        z_sb = sb("z_sb", [P, T, PAIR])
        h_hi = sb("h_hi", [P, T, PAIR], F32R)
        h_lo = sb("h_lo", [P, T, PAIR], F32R)
        bn_in = bil_a[:, 0, 0:4, 0:2 * T].rearrange("p n (k t) -> p n k t", k=2)
        bn_tmp = bil_b[:, 0, 0:3, 0:2 * T].rearrange("p n (k t) -> p n k t", k=2)
        bias_raw = z_sb[0:HALF, 0, :]

        conv_ps = ps("conv_ps", [P, 2, 2 * 512])
        att_ps = ps("att_ps", [P, 2, 512])
        mm_ps = ps("mm_ps", [P, 2, 512])

        params_in = sem("params_in")
        bias_in = sem("bias_in")
        wn_in = [sem(f"wn_in{b}") for b in range(2)]
        ident_zero, ident_done = sem("ident_zero"), sem("ident_done")
        consts_done = sem("consts_done")
        wt_ready, wt_hi, wt_lo = sem("wt_ready"), sem("wt_hi"), sem("wt_lo")
        bn_step, bn_sqrt = sem("bn_step"), sem("bn_sqrt")
        setup_done = sem("setup_done")
        x_ready = [sem(f"x_ready{b}") for b in range(2)]
        res_ready = [sem(f"res_ready{t}") for t in range(T)]
        stored = [sem(f"stored{t}") for t in range(T)]
        bn_done = sem("bn_done")
        fill1, fill2 = sem("fill1"), sem("fill2")
        hi1_done, hi2_done, hih_done = sem("hi1_done"), sem("hi2_done"), sem("hih_done")
        tile_taken = sem("tile_taken")
        exp_done = sem("exp_done")
        pt_taken = sem("pt_taken")
        relu_done = sem("relu_done")
        tap1, tap2 = sem("tap1"), sem("tap2")
        biased, max_done, sum_done, inv_done = sem("biased"), sem("max_done"), sem("sum_done"), sem("inv_done")
        added0 = sem("added0")
        lo1_done, bil_step, bil_done = sem("lo1_done"), sem("bil_step"), sem("bil_done")
        lo2_done, loh_done = sem("lo2_done"), sem("loh_done")
        sub_done, norm_done = sem("sub_done"), sem("norm_done")
        r_done, added1 = sem("r_done"), sem("added1")
        tile_ready, scores_ready, pt_ready = sem("tile_ready"), sem("scores_ready"), sem("pt_ready")
        mlp0_ready = sem("mlp0_ready")

        x_group = x.rearrange("(g b) (p t) h w -> g t p b (h w)", b=G, t=T)
        x_pair = x.rearrange("(n b) (p t) h w -> n t p b (h w)", b=2, t=T)
        out_pair = out.rearrange("(n b) (p t) h w -> n t p b (h w)", b=2, t=T)
        wn_src = [w_qkv_pw[0:C, :], w_qkv_pw[C:2 * C, :], w_qkv_pw[2 * C:3 * C, :], w_out_pw, w_mlp]
        wn = [q_sb[:, :, :].rearrange("p a b -> p (a b)")[:, 0:T * C].rearrange("p (t c) -> p t c", t=T),
              o_pad[:, :, :].rearrange("p a b -> p (a b)")[:, 0:T * C].rearrange("p (t c) -> p t c", t=T)]
        names = ["q", "k", "v", "o", "m"]

        def inner(pad, b, dy=1, dx=1):
            at = dy * PITCH + dx
            tile = pad[:, b, at:]
            return bass.AP(tile.tensor, tile.offset, [tile.ap[0], [PITCH, ROWS], [1, W]])

        def conv(b):
            return conv_ps[:, b, 0:CONV]

        def conv_rows(b):
            return conv(b).rearrange("p (r c) -> p r c", c=W)

        def staged(b):
            full = y_stage[:, b, :]
            return bass.AP(full.tensor, full.offset, [full.ap[0], [(H + 1) * W, G], [1, HW]])

        def flat(ap):
            return ap.rearrange("p b n -> p (b n)")

        s_rows = s_sb[:, :, :, :].rearrange("p r b j -> p (r b) j")[:, :, 0:J]

        block = ctx.enter_context(nc.Block())

        @block.sync
        def _(sp):
            def load_x(g, t):
                need(sp, bn_done, g * T + (t - 1))
                sp.dma_start(x_in[:, t % 2, :, :], x_group[g, t]).then_inc(x_ready[t % 2], 16)

            def load_res(g, p, t):
                need(sp, stored[t], (g * 2 + p) * 16)
                sp.dma_start(res[:, t, :].rearrange("p (b n) -> p b n", b=2),
                             x_pair[g * 2 + p, t]).then_inc(res_ready[t], 16)

            def store(g, p, t):
                sp.wait_ge(added1 if p else added0, g * T + (t + 1))
                sp.dma_start(out_pair[g * 2 + p, t],
                             res[:, t, :].rearrange("p (b n) -> p b n", b=2)).then_inc(stored[t], 16)

            for m in range(2):
                sp.dma_start(wn[m], wn_src[m].rearrange("(p t) c -> p t c", t=T)).then_inc(wn_in[m % 2], 16)
            sp.dma_start(taps1[:, :, :], w_qkv_dw.rearrange("(p t) o a b -> p t (o a b)", t=T)).then_inc(params_in, 16)
            sp.dma_start(taps2[:, :, :], w_out_dw.rearrange("(p t) o a b -> p t (o a b)", t=T)).then_inc(params_in, 16)
            for n, both in enumerate([(bn1_g, bn2_g), (bn1_b, bn2_b), (bn1_m, bn2_m), (bn1_v, bn2_v)]):
                for k, vec in enumerate(both):
                    sp.dma_start(bn_in[:, n, k, :], vec.rearrange("(p t) -> p t", t=T)).then_inc(params_in, 16)
            for t in range(2):
                load_x(0, t)
            for m in range(2, 5):
                sp.wait_ge(wt_ready, 4 * (m - 1))
                sp.dma_start(wn[m % 2], wn_src[m].rearrange("(p t) c -> p t c", t=T)).then_inc(wn_in[m % 2], 16)
            for half in range(2):
                for yy in range(RH):
                    gy = (half * RH + yy) // 2
                    for dup in range(2):
                        src = bass.AP(rel_table.tensor, rel_table.offset + gy * (2 * RH - 1) * HEADS,
                                      [[HEADS, RH], [(2 * RH - 1) * HEADS, RH], [1, RH * HEADS]])
                        at = yy * W + dup
                        dst = bias_raw[at:at + 2 * RH - 1:2, half * J * HEADS:(half + 1) * J * HEADS]
                        sp.dma_start(dst.rearrange("p (a b) -> p a b", a=RH), src).then_inc(bias_in, 16)
            load_x(0, 2)
            load_x(0, 3)
            for t in range(T):
                load_res(0, 0, t)
            load_x(1, 0)
            load_x(1, 1)

            def iteration(i, more):
                conv2_, att, conv1_, out0, out1 = works(i)
                if conv1_:
                    load_x(i + 1, 2)
                    load_x(i + 1, 3)
                if out1:
                    for t in range(T):
                        store(i - 2, 1, t)
                        if out0:
                            load_res(i - 1, 0, t)
                if more:
                    load_x(i + 2, 0)
                    load_x(i + 2, 1)
                if out0:
                    for t in range(T):
                        store(i - 1, 0, t)
                        load_res(i - 1, 1, t)

            iteration(0, True)
            iteration(1, True)
            with sp.Fori(2, GROUPS - 2) as i:
                iteration(i, True)
            for i in range(GROUPS - 2, GROUPS + 2):
                iteration(i, False)
            for t in range(T):
                sp.wait_ge(stored[t], 16 * 2 * GROUPS)

        @block.scalar
        def _(act):
            def norm1(g, t):
                u, b = t // 2, t % 2
                act.wait_ge(x_ready[b], (g * 2 + (u + 1)) * 16)
                need(act, tap1, g * 32 + (16 * u - 1 + b))
                full = x_pad[:, b, PITCH + 1:]
                dst = bass.AP(full.tensor, full.offset, [full.ap[0], [IMG, G], [PITCH, H], [1, W]])
                nc.scalar.activation(dst, x_in[:, b, :, :].rearrange("p b (r c) -> p b r c", c=W), ACT.Identity,
                                     bias=bn_shift[:, 0, t:t + 1], scale=bn_scale[:, 0, t:t + 1]).then_inc(bn_done, 1)

            def first_tap1(g, t):
                u, b = t // 2, t % 2
                if u == 1:
                    act.wait_ge(tap1, g * 32 + (15 + b))
                elif isinstance(g, int) and g == 1:
                    act.wait_ge(tap1, 31 + b)
                elif not (isinstance(g, int) and g == 0):
                    act.wait_ge(tap2, g * 32 + (b - 33))
                act.wait_ge(bn_done, g * T + (t + 1))
                nc.scalar.activation(conv_rows(b), inner(x_pad, b, 0, 0), ACT.Copy,
                                     scale=taps1[:, t, 0:1]).then_inc(fill1, 1)

            def first_tap2(g, t):
                u, b = t // 2, t % 2
                if u == 1:
                    act.wait_ge(tap2, g * 32 + (15 + b))
                elif not (isinstance(g, int) and g == GROUPS - 1):
                    act.wait_ge(tap1, g * 32 + (63 + b))
                else:
                    act.wait_ge(tap2, g * 32 + (b - 1))
                act.wait_ge(tile_taken, tile_no(g, "PV1") + 4)
                nc.scalar.activation(conv_rows(b), inner(o_pad, t, 0, 0), ACT.Copy,
                                     scale=taps2[:, t, 0:1]).then_inc(fill2, 1)

            def high1(g, t):
                u, b = t // 2, t % 2
                act.wait_ge(tap1, g * 32 + (16 * u + 15 + b))
                if not (isinstance(g, int) and g == 0):
                    act.wait_ge(tile_ready, tile_no(g - 1, "Q1") + 4)
                nc.scalar.activation(y_hi[:, t, :].rearrange("p (b n) -> p b n", b=G), staged(b),
                                     ACT.Copy).then_inc(hi1_done, 1)

            def high2(g, t):
                u, b = t // 2, t % 2
                act.wait_ge(tap2, g * 32 + (16 * u + 15 + b))
                if not (isinstance(g, int) and g == 0):
                    act.wait_ge(tile_ready, tile_no(g + 1, "OUT1B") + 2)
                nc.scalar.activation(o_hi[:, t, :].rearrange("p (b n) -> p b n", b=G), staged(b),
                                     ACT.Copy).then_inc(hi2_done, 1)

            def take(i, what, k, dst, src):
                act.wait_ge(tile_ready, tile_no(i, what) + (k + 1))
                nc.scalar.activation(dst, src, ACT.Copy).then_inc(tile_taken, 1)

            def take_k(i, h):
                take(i, "K", h, k_sb[:, h, :], mm_ps[:, h % 2, 0:G * J])

            def take_v(i, p):
                take(i, "V", p, v_sb[:, p, :], mm_ps[:, p, :])

            def take_q(i, p, t):
                take(i, f"Q{p}", t, q_sb[:, t, PAIR * p:PAIR * (p + 1)], mm_ps[:, t % 2, 0:PAIR])

            def take_out(g, p, t):
                if p == 0 and not (isinstance(g, int) and g == 0):
                    act.wait_ge(added1, g * T + (t - 3))
                elif p == 1 and t < 2:
                    act.wait_ge(loh_done, g * 8 + (t + 1))
                act.wait_ge(tile_ready, out_tile(g, p, t) + 1)
                nc.scalar.activation(z_sb[:, t, :], mm_ps[:, t % 2, 0:PAIR], ACT.Copy).then_inc(tile_taken, 1)

            def relu(i, p, t):
                g = i - 1 - p
                act.wait_ge(r_done, g * 8 + (4 * p + t + 1))
                nc.scalar.activation(z_sb[:, t, :], res[:, t, :], ACT.Relu, bias=bn_shift[:, 1, t:t + 1],
                                     scale=bn_scale[:, 1, t:t + 1]).then_inc(relu_done, 1)
                act.wait_ge(relu_done, g * 8 + (4 * p + t + 1))
                if p == 1:
                    act.wait_ge(mlp0_ready, g * T + T)
                elif not (isinstance(i, int) and i == 1):
                    act.wait_ge(tile_ready, tile_no(i, "MLP1") + 4)
                nc.scalar.activation(h_hi[:, t, :], z_sb[:, t, :], ACT.Copy).then_inc(hih_done, 1)

            def take_mlp1(i, t):
                take(i, "MLP1", t, z_sb[:, t, :], mm_ps[:, t % 2, 0:PAIR])

            def exp(i, p):
                act.wait_ge(sub_done, i * 2 + (p + 1))
                nc.scalar.activation(s_rows, s_rows, ACT.Exp, scale=SCALE).then_inc(exp_done, 1)

            def take_pt(i, p):
                act.wait_ge(pt_ready, i * 2 + (p + 1))
                nc.scalar.activation(pt_sb[:, :, :].rearrange("p (a b) n -> p a (b n)", a=2),
                                     att_ps[:, :, 0:PAIR], ACT.Copy).then_inc(pt_taken, 1)

            def take_pv(i, p):
                need(act, tap2, i * 32)
                for hp in range(2):
                    for b in range(2):
                        full = o_pad[:, 2 * hp, PITCH + 1 + IMG * (2 * p + b):]
                        dst = bass.AP(full.tensor, full.offset, [full.ap[0], [PAD, 2], [PITCH, H], [1, W]])
                        take(i, f"PV{p}", 2 * hp + b, dst,
                             mm_ps[:, b, 0:PAIR].rearrange("p (h r c) -> p h r c", h=2, c=W))

            for m, name in enumerate(names):
                for s in range(T):
                    act.wait_ge(wt_ready, 4 * m + s + 1)
                    src = mm_ps[:, s % 2, :].rearrange("p (t n) -> p t n", t=T)
                    if name in w_hi:
                        nc.scalar.activation(w_hi[name][:, s, :, :], src, ACT.Copy).then_inc(wt_hi, 1)
                    else:
                        nc.scalar.activation(w_full[name][:, s, 0:2, :], src[:, 0:2, :], ACT.Copy).then_inc(wt_hi, 1)
            act.wait_ge(bn_step, 1)
            nc.scalar.activation(bn_tmp[:, 1, :, :], bn_tmp[:, 0, :, :], ACT.Sqrt).then_inc(bn_sqrt, 1)
            act.wait_ge(setup_done, 1)
            act.wait_ge(consts_done, 2)

            norm1(0, 0)
            norm1(0, 1)
            first_tap1(0, 0)
            first_tap1(0, 1)
            norm1(0, 2)
            first_tap1(0, 2)
            norm1(0, 3)
            first_tap1(0, 3)
            high1(0, 0)
            high1(0, 1)

            def iteration(i):
                conv2_, att, conv1_, out0, out1 = works(i)
                for b in range(2):
                    if conv2_:
                        first_tap2(i - 1, b)
                    if att:
                        high1(i, 2 + b)
                for b in range(2):
                    if out1:
                        take_out(i - 2, 1, 2 + b)
                    if conv1_:
                        norm1(i + 1, b)
                if att:
                    for t in range(T):
                        take_q(i, 0, t)
                for t in range(T):
                    if att:
                        take_k(i, t)
                    if out1 and t < 2:
                        relu(i, 1, t)
                    if conv2_:
                        if t < 2:
                            first_tap2(i - 1, 2 + t)
                        else:
                            high2(i - 1, t - 2)
                if out1:
                    relu(i, 1, 2)
                    relu(i, 1, 3)
                if att:
                    take_v(i, 0)
                    exp(i, 0)
                    take_v(i, 1)
                if out1:
                    take_mlp1(i, 0)
                    take_mlp1(i, 1)
                for b in range(2):
                    if conv1_:
                        first_tap1(i + 1, b)
                    if out1:
                        take_mlp1(i, 2 + b)
                    if conv2_:
                        high2(i - 1, 2 + b)
                if att:
                    take_pt(i, 0)
                    for t in range(T):
                        take_q(i, 1, t)
                    take_pv(i, 0)
                if out0:
                    take_out(i - 1, 0, 0)
                if att:
                    exp(i, 1)
                if out0:
                    take_out(i - 1, 0, 1)
                for b in range(2):
                    if out0:
                        take_out(i - 1, 0, 2 + b)
                        relu(i, 0, b)
                    if conv1_:
                        norm1(i + 1, 2 + b)
                        first_tap1(i + 1, 2 + b)
                if att:
                    take_pt(i, 1)
                for b in range(2):
                    if out0:
                        relu(i, 0, 2 + b)
                    if conv1_:
                        high1(i + 1, b)
                    if out0:
                        take_out(i - 1, 1, b)
                if att:
                    take_pv(i, 1)

            iteration(0)
            iteration(1)
            with act.Fori(2, GROUPS - 1) as i:
                iteration(i)
            for i in range(GROUPS - 1, GROUPS + 2):
                iteration(i)

        @block.vector
        def _(dve):
            def conv_unit(taps, source, tap_done, filled, g, u, stage_free, between):
                for k in range(2 * STEPS):
                    if k in between:
                        between[k]()
                    b, step = k % 2, k // 2 + 1
                    t = 2 * u + b
                    dy, dx = TAPS[step]
                    if step == 1:
                        dve.wait_ge(filled, g * T + (t + 1))
                    else:
                        dve.wait_ge(tap_done, g * 32 + (16 * u + k - 1))
                    dst = conv(b).rearrange("p (r c) -> p r c", c=W)
                    if step == STEPS:
                        stage_free(b)
                        dst = y_stage[:, b, :].rearrange("p (r c) -> p r c", c=W)
                    nc.vector.scalar_tensor_tensor(
                        out=dst, in0=inner(source, t if source is o_pad else b, dy, dx),
                        scalar=taps[:, t, 3 * dy + dx:3 * dy + dx + 1],
                        in1=conv_rows(b), op0=ALU.mult, op1=ALU.add).then_inc(tap_done, 1)

            def conv1(g, u, between):
                def stage_free(b):
                    if u == 1:
                        dve.wait_ge(bil_done, g * T + (b + 1))
                    elif isinstance(g, int) and g == 1:
                        dve.wait_ge(bil_done, 3 + b)
                    elif not (isinstance(g, int) and g == 0):
                        dve.wait_ge(lo2_done, g * T + (b - 5))
                conv_unit(taps1, x_pad, tap1, fill1, g, u, stage_free, between)

            def conv2(g, u, between):
                def stage_free(b):
                    if u == 1:
                        dve.wait_ge(lo2_done, g * T + (b + 1))
                    elif not (isinstance(g, int) and g == GROUPS - 1):
                        dve.wait_ge(bil_done, g * T + (7 + b))
                    else:
                        dve.wait_ge(lo2_done, g * T + (b - 1))
                conv_unit(taps2, o_pad, tap2, fill2, g, u, stage_free, between)

            def bias_max(i, p):
                for b in range(2):
                    dve.wait_ge(scores_ready, i * 4 + (2 * p + b + 1))
                    if b == 0:
                        need(dve, pt_ready, i * 2 + p)
                    nc.vector.tensor_tensor(s_sb[:, :, b, 0:J], att_ps[0:HALF, b, 0:PAIR].rearrange("p (r j) -> p r j", j=J),
                                            bias[:, :, :, :].rearrange("p a h j -> p (a h) j"),
                                            ALU.add).then_inc(biased, 1)
                dve.wait_ge(biased, i * 4 + (2 * p + 2))
                nc.vector.tensor_reduce(row_max[:, :], s_rows, AX_X, ALU.max).then_inc(max_done, 1)

            def sum_inv(i, p):
                dve.wait_ge(exp_done, i * 2 + (p + 1))
                nc.vector.tensor_reduce(row_sum[:, :], s_rows, AX_X, ALU.add).then_inc(sum_done, 1)
                dve.wait_ge(sum_done, i * 2 + (p + 1))
                nc.vector.reciprocal(row_inv[:, :], row_sum[:, :]).then_inc(inv_done, 1)

            def add_mlp0(i, t):
                dve.wait_ge(mlp0_ready, i * T + (t + 1 - T))
                nc.vector.tensor_tensor(res[:, t, :], mm_ps[:, t % 2, 0:PAIR], res[:, t, :],
                                        ALU.add).then_inc(added0, 1)

            nc.vector.memset(x_pad[:, :, :], 0.0)
            nc.vector.memset(yb[:, :, :, :], 0.0)
            nc.vector.memset(s_sb[:, :, :, :], 0.0).then_inc(consts_done, 1)
            gamma, beta, mean, var = (bn_in[:, n, :, :] for n in range(4))
            a, root, t3 = (bn_tmp[:, n, :, :] for n in range(3))
            dve.wait_ge(params_in, 16 * 10)
            steps = [0]

            def step(instruction):
                steps[0] += 1
                instruction.then_inc(bn_step, 1)
                dve.wait_ge(bn_step, steps[0])

            step(nc.vector.tensor_scalar(a, var, EPS, None, ALU.add))
            for m, name in enumerate(names):
                for s in range(T):
                    dve.wait_ge(wt_ready, 4 * m + s + 1)
                    dve.wait_ge(wt_hi, 4 * m + s + 1)
                    src = mm_ps[:, s % 2, :].rearrange("p (t n) -> p t n", t=T)
                    if name in w_hi:
                        nc.vector.tensor_tensor(w_lo[name][:, s, :, :], src, w_hi[name][:, s, :, :].bitcast(F32),
                                                ALU.subtract).then_inc(wt_lo, 1)
                    else:
                        nc.vector.tensor_copy(w_full[name][:, s, 2:4, :], src[:, 2:4, :]).then_inc(wt_lo, 1)
            nc.vector.memset(o_pad[:, :, :], 0.0)
            dve.wait_ge(bn_sqrt, 1)
            step(nc.vector.reciprocal(t3, root))
            step(nc.vector.tensor_tensor(t3, t3, a, ALU.mult))
            step(nc.vector.tensor_tensor(t3, t3, root, ALU.add))
            step(nc.vector.tensor_scalar(t3, t3, 0.5, None, ALU.mult))
            step(nc.vector.reciprocal(root, t3))
            step(nc.vector.tensor_tensor(bn_scale[:, :, :], root, gamma, ALU.mult))
            step(nc.vector.tensor_tensor(t3, bn_scale[:, :, :], mean, ALU.mult))
            step(nc.vector.tensor_tensor(bn_shift[:, :, :], beta, t3, ALU.subtract))
            dve.wait_ge(bias_in, 16 * 4 * RH)
            for half in range(2):
                raw = bias_raw[:, half * J * HEADS:(half + 1) * J * HEADS]
                backwards = bass.AP(raw.tensor, raw.offset + (J - 1) * HEADS, [raw.ap[0], [1, HEADS], [-HEADS, J]])
                last = nc.vector.tensor_copy(bias[:, half, :, :], backwards)
            step(last)
            nc.vector.memset(row_inv[:, :], 0.0).then_inc(setup_done, 1)

            conv1(0, 0, {})
            conv1(0, 1, {})

            def iteration(i):
                conv2_, att, conv1_, out0, out1 = works(i)
                softmax0 = {4: lambda: bias_max(i, 0), 9: lambda: sum_inv(i, 0)} if att else {}
                if conv2_:
                    conv2(i - 1, 0, {})
                    conv2(i - 1, 1, softmax0)
                elif att:
                    bias_max(i, 0)
                    sum_inv(i, 0)
                if conv1_:
                    conv1(i + 1, 0, {10: lambda: bias_max(i, 1), 15: lambda: sum_inv(i, 1)})
                    conv1(i + 1, 1, {9 + 2 * t: lambda t=t: add_mlp0(i, t) for t in range(T)} if out0 else {})
                else:
                    if att:
                        bias_max(i, 1)
                        sum_inv(i, 1)
                    if out0:
                        for t in range(T):
                            add_mlp0(i, t)

            iteration(0)
            iteration(1)
            with dve.Fori(2, GROUPS - 1) as i:
                iteration(i)
            for i in range(GROUPS - 1, GROUPS + 2):
                iteration(i)

        @block.gpsimd
        def _(pool):
            def low1(g, t):
                b = t % 2
                pool.wait_ge(hi1_done, g * T + (t + 1))
                nc.gpsimd.tensor_tensor(y_lo[:, t, :].rearrange("p (b n) -> p b n", b=G), staged(b),
                                        y_hi[:, t, :].bitcast(F32).rearrange("p (b n) -> p b n", b=G),
                                        ALU.subtract).then_inc(lo1_done, 1)

            def bilinear(g, t):
                full = y_stage[:, t % 2, :]

                def rows(odd):
                    return bass.AP(full.tensor, full.offset + odd * W,
                                   [full.ap[0], [(H + 1) * W, G], [2 * W, RH], [1, W]])

                def by_row(w):
                    f = frac[:, w, :]
                    return bass.AP(f.tensor, f.offset, [f.ap[0], [0, G], [1, RH], [0, W]])

                def by_column(w):
                    f = frac[:, w, :]
                    return bass.AP(f.tensor, f.offset, [f.ap[0], [0, G * RH], [1, RH]])

                columns = bil_a[:, :, :, :].rearrange("p b r c -> p (b r) c")
                left = bil_b[:, 0:2, :, :].rearrange("p b r c -> p (b r c)").rearrange("p (r c) -> p r c", c=RH)
                right = bil_b[:, 2:4, :, :].rearrange("p b r c -> p (b r c)").rearrange("p (r c) -> p r c", c=RH)
                n = g * 20 + 5 * t
                need(pool, bil_done, g * T + t)
                nc.gpsimd.tensor_tensor(bil_a[:, :, :, :], rows(0), by_row(0), ALU.mult).then_inc(bil_step, 1)
                nc.gpsimd.tensor_tensor(bil_b[:, :, :, :], rows(1), by_row(1), ALU.mult).then_inc(bil_step, 1)
                pool.wait_ge(bil_step, n + 2)
                nc.gpsimd.tensor_tensor(bil_a[:, :, :, :], bil_a[:, :, :, :], bil_b[:, :, :, :],
                                        ALU.add).then_inc(bil_step, 1)
                pool.wait_ge(bil_step, n + 3)
                nc.gpsimd.tensor_tensor(left, columns[:, :, 0:W:2], by_column(0), ALU.mult).then_inc(bil_step, 1)
                nc.gpsimd.tensor_tensor(right, columns[:, :, 1:W:2], by_column(1), ALU.mult).then_inc(bil_step, 1)
                pool.wait_ge(bil_step, n + 5)
                nc.gpsimd.tensor_tensor(yb[:, t, :, 0:J], left.rearrange("p (b r) c -> p b (r c)", b=G),
                                        right.rearrange("p (b r) c -> p b (r c)", b=G), ALU.add).then_inc(bil_done, 1)

            def low2(g, t):
                pool.wait_ge(hi2_done, g * T + (t + 1))
                nc.gpsimd.tensor_tensor(o_lo[:, t, :].rearrange("p (b n) -> p b n", b=G), staged(t % 2),
                                        o_hi[:, t, :].bitcast(F32).rearrange("p (b n) -> p b n", b=G),
                                        ALU.subtract).then_inc(lo2_done, 1)

            def wide(row):
                return bass.AP(row[:, :].tensor, row[:, :].offset, [row[:, :].ap[0], [1, 16], [0, J]])

            def less_max(i, p):
                pool.wait_ge(max_done, i * 2 + (p + 1))
                nc.gpsimd.tensor_tensor(s_rows, s_rows, wide(row_max), ALU.subtract).then_inc(sub_done, 1)

            def normalise(i, p):
                pool.wait_ge(inv_done, i * 2 + (p + 1))
                nc.gpsimd.tensor_tensor(s_rows, s_rows, wide(row_inv), ALU.mult).then_inc(norm_done, 1)

            def residual(i, p, t):
                g = i - 1 - p
                pool.wait_ge(res_ready[t], (g * 2 + (p + 1)) * 16)
                pool.wait_ge(tile_taken, out_tile(g, p, t) + 1)
                nc.gpsimd.tensor_tensor(res[:, t, :], z_sb[:, t, :], res[:, t, :], ALU.add).then_inc(r_done, 1)

            def lowh(i, p, t):
                g = i - 1 - p
                pool.wait_ge(hih_done, g * 8 + (4 * p + t + 1))
                nc.gpsimd.tensor_tensor(h_lo[:, t, :], z_sb[:, t, :], h_hi[:, t, :].bitcast(F32),
                                        ALU.subtract).then_inc(loh_done, 1)

            def add_mlp1(i, t):
                pool.wait_ge(tile_taken, tile_no(i, "MLP1") + (t + 1))
                nc.gpsimd.tensor_tensor(res[:, t, :], z_sb[:, t, :], res[:, t, :], ALU.add).then_inc(added1, 1)

            nc.gpsimd.memset(ident[:, :], 0.0).then_inc(ident_zero, 1)
            pool.wait_ge(ident_zero, 1)
            nc.gpsimd.affine_select(out=ident[:, :], in_=ident[:, :], compare_op=ALU.not_equal, fill=1.0, base=0,
                                    pattern=[[-1, P]], channel_multiplier=1).then_inc(ident_done, 1)
            at = np.linspace(0.0, H - 1, RH, dtype=np.float32)
            for j in range(RH):
                w = float(np.float32(at[j] - np.float32(2 * j)))
                nc.gpsimd.memset(frac[:, 0, j:j + 1], float(np.float32(1.0) - np.float32(w)))
                last = nc.gpsimd.memset(frac[:, 1, j:j + 1], w)
            last.then_inc(consts_done, 1)
            pool.wait_ge(consts_done, 2)
            for t in (0, 1):
                low1(0, t)
            for t in (0, 1):
                bilinear(0, t)

            def iteration(i):
                conv2_, att, conv1_, out0, out1 = works(i)
                if att:
                    low1(i, 2)
                    low1(i, 3)
                    bilinear(i, 2)
                    bilinear(i, 3)
                if out1:
                    residual(i, 1, 0)
                    residual(i, 1, 1)
                    lowh(i, 1, 0)
                    residual(i, 1, 2)
                    lowh(i, 1, 1)
                    residual(i, 1, 3)
                    lowh(i, 1, 2)
                    lowh(i, 1, 3)
                if att:
                    less_max(i, 0)
                if conv2_:
                    low2(i - 1, 0)
                if att:
                    normalise(i, 0)
                if conv2_:
                    low2(i - 1, 1)
                if out1:
                    for t in range(T):
                        add_mlp1(i, t)
                if conv2_:
                    low2(i - 1, 2)
                    low2(i - 1, 3)
                if att:
                    less_max(i, 1)
                if out0:
                    residual(i, 0, 0)
                    residual(i, 0, 1)
                    lowh(i, 0, 0)
                if att:
                    normalise(i, 1)
                if out0:
                    residual(i, 0, 2)
                    lowh(i, 0, 1)
                    residual(i, 0, 3)
                    lowh(i, 0, 2)
                    lowh(i, 0, 3)
                if conv1_:
                    for t in (0, 1):
                        low1(i + 1, t)
                        bilinear(i + 1, t)

            iteration(0)
            iteration(1)
            with pool.Fori(2, GROUPS - 1) as i:
                iteration(i)
            for i in range(GROUPS - 1, GROUPS + 2):
                iteration(i)

        @block.tensor
        def _(pe):
            def product(bank, name, hi, lo, s_ready, t, cols):
                for s in range(T):
                    s_ready(s)
                    sides = [(w_hi, hi), (w_hi, lo), (w_lo, hi)]
                    for m, (w, r) in enumerate(sides):
                        last = nc.tensor.matmul(mm_ps[:, bank, 0:PAIR], w[name][:, s, t, :],
                                                r[:, s, cols:cols + PAIR],
                                                start=(s == 0 and m == 0), stop=(s == T - 1 and m == 2))
                return last

            def out_product(g, p, t):
                if p == 1 and t >= 2:
                    pe.wait_ge(added0, g * T + (t + 1))
                else:
                    pe.wait_ge(tile_taken, out_tile(g, p, t) - 1)

                def s_ready(s):
                    if p == 0 and t == 0:
                        pe.wait_ge(lo2_done, g * T + (s + 1))
                product(t % 2, "o", o_hi, o_lo, s_ready, t, PAIR * p).then_inc(tile_ready, 1)

            def mlp(i, p):
                g = i - 1 - p
                for t in range(T):
                    def s_ready(s):
                        if t == 0:
                            pe.wait_ge(loh_done, g * 8 + (4 * p + s + 1))
                    if p == 1:
                        pe.wait_ge(tile_taken, tile_no(i, "MLP1") + (t - 1))
                        product(t % 2, "m", h_hi, h_lo, s_ready, t, 0).then_inc(tile_ready, 1)
                        continue
                    if t < 2:
                        pe.wait_ge(tile_taken, tile_no(i, "END") + (t - 1))
                    else:
                        pe.wait_ge(added0, g * T + (t - 1))
                    product(t % 2, "m", h_hi, h_lo, s_ready, t, 0).then_inc(mlp0_ready, 1)

            def queries(i, p):
                for t in range(T):
                    need(pe, tile_taken, tile_no(i, f"Q{p}") + (t - 1))

                    def s_ready(s):
                        if p == 0 and t == 0:
                            pe.wait_ge(lo1_done, i * T + (s + 1))
                    product(t % 2, "q", y_hi, y_lo, s_ready, t, PAIR * p).then_inc(tile_ready, 1)

            def keys(i):
                for h in range(HEADS):
                    need(pe, tile_taken, tile_no(i, "K") + (h - 1))
                    for s in range(T):
                        if h == 0:
                            pe.wait_ge(bil_done, i * T + (s + 1))
                        last = nc.tensor.matmul(mm_ps[:, h % 2, 0:G * J], w_full["k"][:, s, h, :],
                                                yb[:, s, :, 0:J], start=(s == 0), stop=(s == T - 1))
                    last.then_inc(tile_ready, 1)

            def values(i):
                for p in range(2):
                    pe.wait_ge(tile_taken, tile_no(i, "V") + (p - 1))
                    for s in range(T):
                        last = nc.tensor.matmul(mm_ps[:, p, :],
                                                yb[:, s, 2 * p:2 * p + 2, :].rearrange("p b j -> p (b j)"),
                                                w_full["v"][:, s, :, :].rearrange("p t n -> p (t n)"),
                                                start=(s == 0), stop=(s == T - 1))
                    last.then_inc(tile_ready, 1)

            def scores(i, p):
                pe.wait_ge(tile_taken, tile_no(i, "Q1" if p else "K") + 4)
                need(pe, pt_taken, i * 2 + p)
                for b in range(2):
                    for half in range(2):
                        for h in range(HEADS):
                            at = PAIR * p + HW * b + HALF * half
                            to = (half * HEADS + h) * J
                            last = nc.tensor.matmul(att_ps[0:HALF, b, to:to + J], q_sb[:, h, at:at + HALF],
                                                    k_sb[:, h, J * (2 * p + b):J * (2 * p + b + 1)],
                                                    start=True, stop=True)
                    last.then_inc(scores_ready, 1)

            def turn(i, p):
                pe.wait_ge(norm_done, i * 2 + (p + 1))
                for half in range(2):
                    for h in range(HEADS):
                        both = s_sb[:, half * HEADS + h, :, :].rearrange("p b j -> p (b j)")
                        at = HW * (h % 2) + HALF * half
                        last = nc.tensor.transpose(att_ps[:, h // 2, at:at + HALF], both, ident[0:HALF, 0:HALF])
                last.then_inc(pt_ready, 1)

            def attend(i, p):
                pe.wait_ge(pt_taken, i * 2 + (p + 1))
                for h in range(HEADS):
                    for b in range(2):
                        if h % 2 == 0:
                            pe.wait_ge(tile_taken, tile_no(i, f"PV{p}") + (h + b - 1))
                        mm = nc.tensor.matmul(mm_ps[:, b, HW * (h % 2):HW * (h % 2 + 1)],
                                              v_sb[JP * b:JP * b + J, p, DH * h:DH * (h + 1)],
                                              pt_sb[JP * b:JP * b + J, h, :], start=True, stop=True)
                        if h % 2:
                            mm.then_inc(tile_ready, 1)

            pe.wait_ge(ident_done, 1)
            for m in range(5):
                pe.wait_ge(wn_in[m % 2], 16 * (m // 2 + 1))
                for s in range(T):
                    n = 4 * m + s
                    need(pe, wt_hi, n - 1)
                    need(pe, wt_lo, n - 1)
                    for t in range(T):
                        last = nc.tensor.transpose(mm_ps[:, s % 2, P * t:P * (t + 1)], wn[m % 2][:, t, s:C:T],
                                                   ident[:, :])
                    last.then_inc(wt_ready, 1)
            pe.wait_ge(wt_hi, 20)
            pe.wait_ge(wt_lo, 20)

            def iteration(i):
                conv2_, att, conv1_, out0, out1 = works(i)
                if out1:
                    out_product(i - 2, 1, 2)
                    out_product(i - 2, 1, 3)
                if att:
                    queries(i, 0)
                    keys(i)
                    scores(i, 0)
                    values(i)
                if out1:
                    mlp(i, 1)
                if att:
                    turn(i, 0)
                    queries(i, 1)
                    attend(i, 0)
                    scores(i, 1)
                if out0:
                    for t in range(T):
                        out_product(i - 1, 0, t)
                if att:
                    turn(i, 1)
                if out0:
                    out_product(i - 1, 1, 0)
                    out_product(i - 1, 1, 1)
                if att:
                    attend(i, 1)
                if out0:
                    mlp(i, 0)

            iteration(0)
            iteration(1)
            with pe.Fori(2, GROUPS - 1) as i:
                iteration(i)
            for i in range(GROUPS - 1, GROUPS + 2):
                iteration(i)


_INS = ['x', 'L0_conv_bn1_g', 'L0_conv_bn1_b', 'L0_conv_bn1_m', 'L0_conv_bn1_v', 'L0_conv_w_qkv_dw',
        'L0_conv_w_qkv_pw', 'L0_conv_rel_table', 'L0_conv_w_out_dw', 'L0_conv_w_out_pw', 'L0_conv_bn2_g',
        'L0_conv_bn2_b', 'L0_conv_bn2_m', 'L0_conv_bn2_v', 'L0_conv_w_mlp']
_OUTS = [((B, C, H, W), 'float32')]


def kernel(**inputs):
    import numpy as _np
    import concourse.bacc as _bacc
    from concourse import mybir as _mybir
    from concourse.bass_utils import run_bass_kernel_spmd as _run

    nc = _bacc.Bacc("TRN2", target_bir_lowering=False, num_devices=1)
    arrays, args = {}, []
    for name in _INS:
        a = _np.ascontiguousarray(inputs[name])
        arrays[f"in_{name}_dram"] = a
        args.append(nc.dram_tensor(f"in_{name}_dram", a.shape, _mybir.dt.from_np(a.dtype), kind="ExternalInput").ap())
    for i, (shape, dtype) in enumerate(_OUTS):
        dt = _mybir.dt.from_np(_np.dtype(dtype))
        args.append(nc.dram_tensor(f"out_{i}_dram", shape, dt, kind="ExternalOutput").ap())
    build(nc, *args)
    r = _run(nc, [arrays], core_ids=[0])
    got = tuple(r.results[0][f"out_{i}_dram"] for i in range(len(_OUTS)))
    return got[0]
```

```python
from contextlib import ExitStack

import numpy as np

import concourse.bass as bass
from concourse import mybir

F32 = mybir.dt.float32
F32R = mybir.dt.float32r
ALU = mybir.AluOpType
ACT = mybir.ActivationFunctionType
AX_X = mybir.AxisListType.X

P = 128
B, C, H, W = 128, 512, 14, 14
T = C // P
HEADS, DH = 4, C // 4
HW = H * W
RH = 7
J = RH * RH
JP = 64
EPS = 1e-5
SCALE = DH ** (-0.5)
G = 4
GROUPS = B // G
PITCH = W + 1
ROW = G * PITCH
TILE = (H + 1) * ROW
SPLIT_FIRST = 8
TAPS = [(dy, dx) for dy in range(3) for dx in range(3)]
STEPS = len(TAPS) - 1
PAIR = 2 * HW
GHW = G * HW
HALF = HW // 2


def need(engine, semaphore, count):
    if isinstance(count, int) and count <= 0:
        return
    engine.wait_ge(semaphore, count)


ORDER = ["OUT1B", "Q0", "Q0+", "V", "K", "K+", "Q1", "MLP1", "Q1+", "MLP1+", "OUT0", "PV0", "OUT0+",
         "OUT1A", "PV0+", "MLP0", "PV1", "PV1+", "MLP0+"]


def works(i):
    if not isinstance(i, int):
        return True, True, True, True, True
    return 1 <= i <= GROUPS, i < GROUPS, i < GROUPS - 1, 1 <= i <= GROUPS, i >= 2


def stages(i):
    _, att, _, out0, out1 = works(i)
    has = {"OUT1B": out1, "MLP1": out1, "OUT0": out0, "OUT1A": out0, "MLP0": out0}
    return [stage for stage in ORDER if has.get(stage.rstrip("+"), att)]


def counted(names):
    return 2 * sum(not stage.startswith("MLP0") for stage in names)


LOOP_TILES = counted(ORDER)
BEFORE_LOOP = counted(stages(0)) + counted(stages(1))


def tile_no(i, what, t=0):
    if t >= 2:
        what, t = what + "+", t - 2
    if isinstance(i, int):
        names = stages(i)
        return sum(counted(stages(n)) for n in range(i)) + counted(names[:names.index(what)]) + t
    return i * LOOP_TILES + (BEFORE_LOOP - 2 * LOOP_TILES + counted(ORDER[:ORDER.index(what)]) + t)


def out_tile(g, p, t):
    if p == 0:
        return tile_no(g + 1, "OUT0", t)
    return tile_no(g + 1, "OUT1A", t) if t < 2 else tile_no(g + 2, "OUT1B", t - 2)


def build(nc, x, bn1_g, bn1_b, bn1_m, bn1_v, w_qkv_dw, w_qkv_pw, rel_table, w_out_dw, w_out_pw,
          bn2_g, bn2_b, bn2_m, bn2_v, w_mlp, out):
    with ExitStack() as ctx:
        def sb(name, shape, dt=F32):
            return ctx.enter_context(nc.sbuf_tensor(name, shape, dt))

        def ps(name, shape):
            return ctx.enter_context(nc.psum_tensor(name, shape, F32))

        def sem(name):
            return ctx.enter_context(nc.semaphore(name))

        w_hi = {m: sb(f"w{m}_hi", [P, T, T, P], F32R) for m in ("q", "o", "m")}
        w_lo = {m: sb(f"w{m}_lo", [P, T, T, P], F32R) for m in ("q", "o", "m")}
        w_full = {m: sb(f"w{m}", [P, T, T, P]) for m in ("k", "v")}
        ident = sb("ident", [P, P])
        taps1 = sb("taps1", [P, T, 9])
        taps2 = sb("taps2", [P, T, 9])
        bn_scale = sb("bn_scale", [P, 2, T])
        bn_shift = sb("bn_shift", [P, 2, T])
        bias = sb("bias", [HALF, 2, HEADS, J])
        frac = sb("frac", [P, 2, RH])

        x_in = sb("x_in", [P, 2, G, HW])
        x_pad = sb("x_pad", [P, 2 * TILE + ROW + 1])
        y_stage = sb("y_stage", [P, 2, GHW])
        y_hi = sb("y_hi", [P, T, GHW], F32R)
        y_lo = sb("y_lo", [P, T, GHW], F32R)
        bil_a = sb("bil_a", [P, G, RH, W])
        bil_b = sb("bil_b", [P, G, RH, W])
        yb = sb("yb", [P, T, G, JP])
        q_sb = sb("q_sb", [P, HEADS, GHW])
        k_sb = sb("k_sb", [P, HEADS, G * J])
        v_sb = sb("v_sb", [P, 2, C])
        s_sb = sb("s_sb", [HALF, 2 * HEADS, 2, JP])
        row_max = sb("row_max", [HALF, 16])
        row_sum = sb("row_sum", [HALF, 16])
        row_inv = sb("row_inv", [HALF, 16])
        pt_sb = sb("pt_sb", [P, HEADS, HW])
        o_pad = sb("o_pad", [P, HEADS * TILE + ROW + 1])
        o_hi = sb("o_hi", [P, T, GHW], F32R)
        o_lo = sb("o_lo", [P, T, GHW], F32R)
        res = sb("res", [P, T, PAIR])
        z_sb = sb("z_sb", [P, T, PAIR])
        h_hi = sb("h_hi", [P, T, PAIR], F32R)
        h_lo = sb("h_lo", [P, T, PAIR], F32R)
        bn_in = bil_a[:, 0, 0:4, 0:2 * T].rearrange("p n (k t) -> p n k t", k=2)
        bn_tmp = bil_b[:, 0, 0:3, 0:2 * T].rearrange("p n (k t) -> p n k t", k=2)
        bias_raw = z_sb[0:HALF, 0, :]

        conv_ps = ps("conv_ps", [P, 2, 2 * 512])
        att_ps = ps("att_ps", [P, 2, 512])
        mm_ps = ps("mm_ps", [P, 2, 512])

        params_in = sem("params_in")
        bias_in = sem("bias_in")
        wn_in = [sem(f"wn_in{b}") for b in range(2)]
        ident_zero, ident_done = sem("ident_zero"), sem("ident_done")
        consts_done = sem("consts_done")
        wt_ready, wt_hi, wt_lo = sem("wt_ready"), sem("wt_hi"), sem("wt_lo")
        bn_step, bn_sqrt = sem("bn_step"), sem("bn_sqrt")
        setup_done = sem("setup_done")
        x_ready = [sem(f"x_ready{b}") for b in range(2)]
        res_ready = [sem(f"res_ready{t}") for t in range(T)]
        stored = [sem(f"stored{t}") for t in range(T)]
        bn_done = sem("bn_done")
        fill1, fill2 = sem("fill1"), sem("fill2")
        hi1_done, hi2_done, hih_done = sem("hi1_done"), sem("hi2_done"), sem("hih_done")
        tile_taken = sem("tile_taken")
        exp_done = sem("exp_done")
        pt_taken = sem("pt_taken")
        relu_done = sem("relu_done")
        tap1, tap2 = sem("tap1"), sem("tap2")
        biased, max_done, sum_done, inv_done = sem("biased"), sem("max_done"), sem("sum_done"), sem("inv_done")
        added0 = sem("added0")
        lo1_done, bil_step, bil_done = sem("lo1_done"), sem("bil_step"), sem("bil_done")
        lo2_done, loh_done = sem("lo2_done"), sem("loh_done")
        sub_done, norm_done = sem("sub_done"), sem("norm_done")
        r_done, added1 = sem("r_done"), sem("added1")
        tile_ready, scores_ready, pt_ready = sem("tile_ready"), sem("scores_ready"), sem("pt_ready")
        mlp0_ready = sem("mlp0_ready")

        x_group = x.rearrange("(g b) (p t) h w -> g t p b (h w)", b=G, t=T)
        x_pair = x.rearrange("(n b) (p t) h w -> n t p b (h w)", b=2, t=T)
        out_pair = out.rearrange("(n b) (p t) h w -> n t p b (h w)", b=2, t=T)
        wn_src = [w_qkv_pw[0:C, :], w_qkv_pw[C:2 * C, :], w_qkv_pw[2 * C:3 * C, :], w_out_pw, w_mlp]
        wn = [q_sb[:, :, :].rearrange("p a b -> p (a b)")[:, 0:T * C].rearrange("p (t c) -> p t c", t=T),
              o_pad[:, 0:T * C].rearrange("p (t c) -> p t c", t=T)]
        names = ["q", "k", "v", "o", "m"]

        def inner(pad, b, dy, dx):
            tile = pad[:, b * TILE + dy * ROW + dx:]
            return bass.AP(tile.tensor, tile.offset, [tile.ap[0], [PITCH, H * G], [1, W]])

        def conv_rows(b):
            return conv_ps[:, b, 0:GHW].rearrange("p (r c) -> p r c", c=W)

        def staged(b):
            return y_stage[:, b, :].rearrange("p (r b c) -> p b r c", b=G, c=W)

        def by_image(ap):
            return ap.rearrange("p (b r c) -> p b r c", b=G, c=W)

        s_rows = s_sb[:, :, :, :].rearrange("p r b j -> p (r b) j")[:, :, 0:J]

        block = ctx.enter_context(nc.Block())

        @block.sync
        def _(sp):
            def load_x(g, t):
                need(sp, bn_done, g * T + (t - 1))
                sp.dma_start(x_in[:, t % 2, :, :], x_group[g, t]).then_inc(x_ready[t % 2], 16)

            def load_res(g, p, t):
                need(sp, stored[t], (g * 2 + p) * 16)
                sp.dma_start(res[:, t, :].rearrange("p (b n) -> p b n", b=2),
                             x_pair[g * 2 + p, t]).then_inc(res_ready[t], 16)

            def store(g, p, t):
                sp.wait_ge(added1 if p else added0, g * T + (t + 1))
                sp.dma_start(out_pair[g * 2 + p, t],
                             res[:, t, :].rearrange("p (b n) -> p b n", b=2)).then_inc(stored[t], 16)

            def load_weights(m):
                need(sp, wt_ready, 4 * (m - 1))
                sp.dma_start(wn[m % 2], wn_src[m].rearrange("(p t) c -> p t c", t=T)).then_inc(wn_in[m % 2], 16)

            load_x(0, 0)
            load_x(0, 1)
            for n, both in enumerate([(bn1_g, bn2_g), (bn1_b, bn2_b), (bn1_m, bn2_m), (bn1_v, bn2_v)]):
                for k, vec in enumerate(both):
                    sp.dma_start(bn_in[:, n, k, :], vec.rearrange("(p t) -> p t", t=T)).then_inc(params_in, 16)
            for taps, kernels in ((taps1, w_qkv_dw), (taps2, w_out_dw)):
                sp.dma_start(taps[:, :, :],
                             kernels.rearrange("(p t) o a b -> p t (o a b)", t=T)).then_inc(params_in, 16)
            for m in range(2):
                sp.dma_start(wn[m], wn_src[m].rearrange("(p t) c -> p t c", t=T)).then_inc(wn_in[m], 16)
            load_x(0, 2)
            load_x(0, 3)
            for m in range(2, 5):
                load_weights(m)
            for half in range(2):
                for yy in range(RH):
                    gy = (half * RH + yy) // 2
                    for dup in range(2):
                        src = bass.AP(rel_table.tensor, rel_table.offset + gy * (2 * RH - 1) * HEADS,
                                      [[HEADS, RH], [(2 * RH - 1) * HEADS, RH], [1, RH * HEADS]])
                        at = yy * W + dup
                        dst = bias_raw[at:at + 2 * RH - 1:2, half * J * HEADS:(half + 1) * J * HEADS]
                        sp.dma_start(dst.rearrange("p (a b) -> p a b", a=RH), src).then_inc(bias_in, 16)
            for t in range(T):
                load_res(0, 0, t)
            load_x(1, 0)
            load_x(1, 1)

            def iteration(i, more):
                conv2_, att, conv1_, out0, out1 = works(i)
                if conv1_:
                    load_x(i + 1, 2)
                    load_x(i + 1, 3)
                for t in range(T + 1):
                    if out1 and t < T:
                        store(i - 2, 1, t)
                    if out1 and out0 and t > 0:
                        load_res(i - 1, 0, t - 1)
                if more:
                    load_x(i + 2, 0)
                    load_x(i + 2, 1)
                for t in range(T + 1):
                    if out0 and t < T:
                        store(i - 1, 0, t)
                    if out0 and t > 0:
                        load_res(i - 1, 1, t - 1)

            iteration(0, True)
            iteration(1, True)
            with sp.Fori(2, GROUPS - 2) as i:
                iteration(i, True)
            for i in range(GROUPS - 2, GROUPS + 2):
                iteration(i, False)
            for t in range(T):
                sp.wait_ge(stored[t], 16 * 2 * GROUPS)

        @block.scalar
        def _(act):
            def norm1(g, t):
                u, b = t // 2, t % 2
                act.wait_ge(x_ready[b], (g * 2 + (u + 1)) * 16)
                need(act, tap1, g * 32 + (16 * u - 1 + b))
                full = x_pad[:, b * TILE + ROW + 1:]
                dst = bass.AP(full.tensor, full.offset, [full.ap[0], [PITCH, G], [ROW, H], [1, W]])
                nc.scalar.activation(dst, x_in[:, b, :, :].rearrange("p b (r c) -> p b r c", c=W), ACT.Identity,
                                     bias=bn_shift[:, 0, t:t + 1], scale=bn_scale[:, 0, t:t + 1]).then_inc(bn_done, 1)

            def first_tap1(g, t):
                u, b = t // 2, t % 2
                if u == 1:
                    act.wait_ge(tap1, g * 32 + (15 + b))
                elif isinstance(g, int) and g == 1:
                    act.wait_ge(tap1, 31 + b)
                elif not (isinstance(g, int) and g == 0):
                    act.wait_ge(tap2, g * 32 + (b - 33))
                act.wait_ge(bn_done, g * T + (t + 1))
                nc.scalar.activation(conv_rows(b), inner(x_pad, b, 0, 0), ACT.Copy,
                                     scale=taps1[:, t, 0:1]).then_inc(fill1, 1)

            def first_tap2(g, t):
                u, b = t // 2, t % 2
                if u == 1:
                    act.wait_ge(tap2, g * 32 + (15 + b))
                elif not (isinstance(g, int) and g == GROUPS - 1):
                    act.wait_ge(tap1, g * 32 + (63 + b))
                else:
                    act.wait_ge(tap2, g * 32 + (b - 1))
                act.wait_ge(tile_taken, tile_no(g, "PV1", 3) + 1)
                nc.scalar.activation(conv_rows(b), inner(o_pad, t, 0, 0), ACT.Copy,
                                     scale=taps2[:, t, 0:1]).then_inc(fill2, 1)

            def high1(g, t):
                u, b = t // 2, t % 2
                act.wait_ge(tap1, g * 32 + (16 * u + 15 + b))
                if not (isinstance(g, int) and g == 0):
                    act.wait_ge(tile_ready, tile_no(g - 1, "Q1", 3) + 1)
                nc.scalar.activation(by_image(y_hi[:, t, :]), staged(b),
                                     ACT.Copy).then_inc(hi1_done, 1)

            def high2(g, t):
                u, b = t // 2, t % 2
                act.wait_ge(tap2, g * 32 + (16 * u + 15 + b))
                if not (isinstance(g, int) and g == 0):
                    act.wait_ge(tile_ready, tile_no(g + 1, "OUT1B") + 2)
                nc.scalar.activation(by_image(o_hi[:, t, :]), staged(b),
                                     ACT.Copy).then_inc(hi2_done, 1)

            def take(i, what, k, dst, src):
                act.wait_ge(tile_ready, tile_no(i, what, k) + 1)
                nc.scalar.activation(dst, src, ACT.Copy).then_inc(tile_taken, 1)

            def take_k(i, h):
                take(i, "K", h, k_sb[:, h, :], mm_ps[:, h % 2, 0:G * J])

            def take_v(i, p):
                take(i, "V", p, v_sb[:, p, :], mm_ps[:, p, :])

            def take_q(i, p, t):
                take(i, f"Q{p}", t, q_sb[:, t, PAIR * p:PAIR * (p + 1)], mm_ps[:, t % 2, 0:PAIR])

            def take_out(g, p, t):
                if p == 0 and not (isinstance(g, int) and g == 0):
                    act.wait_ge(added1, g * T + (t - 3))
                elif p == 1 and t < 2:
                    act.wait_ge(loh_done, g * 8 + (t + 1))
                act.wait_ge(tile_ready, out_tile(g, p, t) + 1)
                nc.scalar.activation(z_sb[:, t, :], mm_ps[:, t % 2, 0:PAIR], ACT.Copy).then_inc(tile_taken, 1)

            def relu(i, p, t):
                g = i - 1 - p
                act.wait_ge(r_done, g * 8 + (4 * p + t + 1))
                nc.scalar.activation(z_sb[:, t, :], res[:, t, :], ACT.Relu, bias=bn_shift[:, 1, t:t + 1],
                                     scale=bn_scale[:, 1, t:t + 1]).then_inc(relu_done, 1)

            def highh(i, p, t):
                g = i - 1 - p
                act.wait_ge(relu_done, g * 8 + (4 * p + t + 1))
                if p == 1:
                    act.wait_ge(mlp0_ready, g * T + T)
                elif not (isinstance(i, int) and i == 1):
                    act.wait_ge(tile_ready, tile_no(i, "MLP1", 3) + 1)
                nc.scalar.activation(h_hi[:, t, :], z_sb[:, t, :], ACT.Copy).then_inc(hih_done, 1)

            def take_mlp1(i, t):
                take(i, "MLP1", t, z_sb[:, t, :], mm_ps[:, t % 2, 0:PAIR])

            def exp(i, p):
                act.wait_ge(sub_done, i * 2 + (p + 1))
                nc.scalar.activation(s_rows, s_rows, ACT.Exp, scale=SCALE).then_inc(exp_done, 1)

            def take_pt(i, p):
                act.wait_ge(pt_ready, i * 2 + (p + 1))
                nc.scalar.activation(pt_sb[:, :, :].rearrange("p (a b) n -> p a (b n)", a=2),
                                     att_ps[:, :, 0:PAIR], ACT.Copy).then_inc(pt_taken, 1)

            def take_pv(i, p, hp, b):
                need(act, tap2, i * 32)
                full = o_pad[:, 2 * hp * TILE + ROW + 1 + PITCH * (2 * p + b):]
                dst = bass.AP(full.tensor, full.offset, [full.ap[0], [TILE, 2], [ROW, H], [1, W]])
                take(i, f"PV{p}", 2 * hp + b, dst,
                     mm_ps[:, b, 0:PAIR].rearrange("p (h r c) -> p h r c", h=2, c=W))

            def high_weights(n):
                name, s = names[n // T], n % T
                act.wait_ge(wt_ready, n + 1)
                src = mm_ps[:, s % 2, :].rearrange("p (t n) -> p t n", t=T)
                if name in w_hi:
                    nc.scalar.activation(w_hi[name][:, s, :, :], src, ACT.Copy).then_inc(wt_hi, 1)
                else:
                    nc.scalar.activation(w_full[name][:, s, 0:2, :], src[:, 0:2, :], ACT.Copy).then_inc(wt_hi, 1)

            act.wait_ge(bn_step, 1)
            nc.scalar.activation(bn_tmp[:, 1, :, :], bn_tmp[:, 0, :, :], ACT.Sqrt).then_inc(bn_sqrt, 1)
            act.wait_ge(setup_done, 1)
            norm1(0, 0)
            norm1(0, 1)
            first_tap1(0, 0)
            first_tap1(0, 1)
            for n in range(SPLIT_FIRST):
                high_weights(n)
            norm1(0, 2)
            norm1(0, 3)
            first_tap1(0, 2)
            first_tap1(0, 3)
            high1(0, 0)
            high1(0, 1)
            for n in range(SPLIT_FIRST, 5 * T):
                high_weights(n)
            act.wait_ge(consts_done, 2)

            def iteration(i):
                conv2_, att, conv1_, out0, out1 = works(i)
                if isinstance(i, int) and i == 0:
                    high1(0, 2)
                    high1(0, 3)
                    norm1(1, 0)
                    norm1(1, 1)
                    first_tap1(1, 0)
                    first_tap1(1, 1)
                    take_q(0, 0, 0)
                    take_q(0, 0, 1)
                    take_q(0, 0, 2)
                    take_q(0, 0, 3)
                    take_v(0, 0)
                    norm1(1, 2)
                    norm1(1, 3)
                    take_v(0, 1)
                    first_tap1(1, 2)
                    first_tap1(1, 3)
                    take_k(0, 0)
                    take_k(0, 1)
                    take_k(0, 2)
                    take_k(0, 3)
                    take_q(0, 1, 0)
                    take_q(0, 1, 1)
                    exp(0, 0)
                    take_q(0, 1, 2)
                    take_q(0, 1, 3)
                    take_pt(0, 0)
                    high1(1, 0)
                    take_pv(0, 0, 0, 0)
                    take_pv(0, 0, 0, 1)
                    exp(0, 1)
                    take_pv(0, 0, 1, 0)
                    take_pv(0, 0, 1, 1)
                    high1(1, 1)
                    take_pt(0, 1)
                    take_pv(0, 1, 0, 0)
                    take_pv(0, 1, 0, 1)
                    take_pv(0, 1, 1, 0)
                    take_pv(0, 1, 1, 1)
                    return
                if att:
                    high1(i, 2)
                if conv2_:
                    first_tap2(i - 1, 0)
                    first_tap2(i - 1, 1)
                if att:
                    high1(i, 3)
                if out1:
                    take_out(i - 2, 1, 2)
                    take_out(i - 2, 1, 3)
                if att:
                    take_q(i, 0, 0)
                    take_q(i, 0, 1)
                if out1:
                    relu(i, 1, 0)
                if att:
                    take_q(i, 0, 2)
                    take_q(i, 0, 3)
                if conv2_:
                    first_tap2(i - 1, 2)
                    first_tap2(i - 1, 3)
                if att:
                    take_v(i, 0)
                if conv2_:
                    high2(i - 1, 0)
                if att:
                    take_v(i, 1)
                if out1:
                    relu(i, 1, 1)
                    highh(i, 1, 0)
                if att:
                    take_k(i, 0)
                    take_k(i, 1)
                    take_k(i, 2)
                if out1:
                    highh(i, 1, 1)
                if att:
                    take_k(i, 3)
                if out1:
                    relu(i, 1, 2)
                    highh(i, 1, 2)
                if conv2_:
                    high2(i - 1, 1)
                if att:
                    take_q(i, 1, 0)
                if conv1_:
                    norm1(i + 1, 0)
                if out1:
                    relu(i, 1, 3)
                if att:
                    take_q(i, 1, 1)
                if out1:
                    highh(i, 1, 3)
                if conv1_:
                    norm1(i + 1, 1)
                    first_tap1(i + 1, 0)
                if conv2_:
                    high2(i - 1, 2)
                if conv1_:
                    first_tap1(i + 1, 1)
                if out1:
                    take_mlp1(i, 0)
                    take_mlp1(i, 1)
                if att:
                    exp(i, 0)
                if conv2_:
                    high2(i - 1, 3)
                if att:
                    take_q(i, 1, 2)
                    take_q(i, 1, 3)
                if out1:
                    take_mlp1(i, 2)
                    take_mlp1(i, 3)
                if att:
                    take_pt(i, 0)
                if out0:
                    take_out(i - 1, 0, 0)
                    relu(i, 0, 0)
                    take_out(i - 1, 0, 1)
                    highh(i, 0, 0)
                if conv1_:
                    high1(i + 1, 0)
                if att:
                    take_pv(i, 0, 0, 0)
                if out0:
                    relu(i, 0, 1)
                if att:
                    take_pv(i, 0, 0, 1)
                if conv1_:
                    norm1(i + 1, 2)
                    norm1(i + 1, 3)
                    first_tap1(i + 1, 2)
                if out0:
                    take_out(i - 1, 0, 2)
                if conv1_:
                    first_tap1(i + 1, 3)
                if out0:
                    highh(i, 0, 1)
                if att:
                    exp(i, 1)
                if out0:
                    take_out(i - 1, 0, 3)
                    relu(i, 0, 2)
                    highh(i, 0, 2)
                    take_out(i - 1, 1, 0)
                    relu(i, 0, 3)
                    take_out(i - 1, 1, 1)
                    highh(i, 0, 3)
                if att:
                    take_pv(i, 0, 1, 0)
                    take_pv(i, 0, 1, 1)
                if conv1_:
                    high1(i + 1, 1)
                if att:
                    take_pt(i, 1)
                    take_pv(i, 1, 0, 0)
                    take_pv(i, 1, 0, 1)
                    take_pv(i, 1, 1, 0)
                    take_pv(i, 1, 1, 1)

            iteration(0)
            iteration(1)
            with act.Fori(2, GROUPS - 1) as i:
                iteration(i)
            for i in range(GROUPS - 1, GROUPS + 2):
                iteration(i)

        @block.vector
        def _(dve):
            def conv_unit(taps, source, tap_done, filled, g, u, stage_free, between):
                for k in range(2 * STEPS):
                    for other in between.get(k, ()):
                        other()
                    b, step = k % 2, k // 2 + 1
                    t = 2 * u + b
                    dy, dx = TAPS[step]
                    if step == 1:
                        dve.wait_ge(filled, g * T + (t + 1))
                    else:
                        dve.wait_ge(tap_done, g * 32 + (16 * u + k - 1))
                    dst = conv_rows(b)
                    if step == STEPS:
                        stage_free(b)
                        dst = y_stage[:, b, :].rearrange("p (r c) -> p r c", c=W)
                    nc.vector.scalar_tensor_tensor(
                        out=dst, in0=inner(source, t if source is o_pad else b, dy, dx),
                        scalar=taps[:, t, 3 * dy + dx:3 * dy + dx + 1],
                        in1=conv_rows(b), op0=ALU.mult, op1=ALU.add).then_inc(tap_done, 1)
                for other in between.get(2 * STEPS, ()):
                    other()

            def conv1(g, u, between):
                def stage_free(b):
                    if u == 1:
                        dve.wait_ge(bil_done, g * T + (b + 1))
                    elif isinstance(g, int) and g == 1:
                        dve.wait_ge(bil_done, 3 + b)
                    elif not (isinstance(g, int) and g == 0):
                        dve.wait_ge(lo2_done, g * T + (b - 5))
                conv_unit(taps1, x_pad, tap1, fill1, g, u, stage_free, between)

            def conv2(g, u, between):
                def stage_free(b):
                    if u == 1:
                        dve.wait_ge(lo2_done, g * T + (b + 1))
                    elif not (isinstance(g, int) and g == GROUPS - 1):
                        dve.wait_ge(bil_done, g * T + (7 + b))
                    else:
                        dve.wait_ge(lo2_done, g * T + (b - 1))
                conv_unit(taps2, o_pad, tap2, fill2, g, u, stage_free, between)

            def add_bias(i, p, b):
                dve.wait_ge(scores_ready, i * 4 + (2 * p + b + 1))
                need(dve, pt_ready, i * 2 + p)
                nc.vector.tensor_tensor(s_sb[:, :, b, 0:J],
                                        att_ps[0:HALF, b, 0:PAIR].rearrange("p (r j) -> p r j", j=J),
                                        bias[:, :, :, :].rearrange("p a h j -> p (a h) j"),
                                        ALU.add).then_inc(biased, 1)

            def maximum(i, p):
                dve.wait_ge(biased, i * 4 + (2 * p + 2))
                nc.vector.tensor_reduce(row_max[:, :], s_rows, AX_X, ALU.max).then_inc(max_done, 1)

            def total(i, p):
                dve.wait_ge(exp_done, i * 2 + (p + 1))
                nc.vector.tensor_reduce(row_sum[:, :], s_rows, AX_X, ALU.add).then_inc(sum_done, 1)

            def invert(i, p):
                dve.wait_ge(sum_done, i * 2 + (p + 1))
                nc.vector.reciprocal(row_inv[:, :], row_sum[:, :]).then_inc(inv_done, 1)

            def add_mlp0(i, t):
                dve.wait_ge(mlp0_ready, i * T + (t + 1 - T))
                nc.vector.tensor_tensor(res[:, t, :], mm_ps[:, t % 2, 0:PAIR], res[:, t, :],
                                        ALU.add).then_inc(added0, 1)

            def low_weights(n):
                name, s = names[n // T], n % T
                dve.wait_ge(wt_ready, n + 1)
                dve.wait_ge(wt_hi, n + 1)
                src = mm_ps[:, s % 2, :].rearrange("p (t n) -> p t n", t=T)
                if name in w_hi:
                    nc.vector.tensor_tensor(w_lo[name][:, s, :, :], src, w_hi[name][:, s, :, :].bitcast(F32),
                                            ALU.subtract).then_inc(wt_lo, 1)
                else:
                    nc.vector.tensor_copy(w_full[name][:, s, 2:4, :], src[:, 2:4, :]).then_inc(wt_lo, 1)

            nc.vector.memset(x_pad[:, :], 0.0)
            nc.vector.memset(row_inv[:, :], 0.0)
            gamma, beta, mean, var = (bn_in[:, n, :, :] for n in range(4))
            a, root, t3 = (bn_tmp[:, n, :, :] for n in range(3))
            dve.wait_ge(params_in, 16 * 10)
            steps = [0]

            def step(instruction):
                steps[0] += 1
                instruction.then_inc(bn_step, 1)
                dve.wait_ge(bn_step, steps[0])

            step(nc.vector.tensor_scalar(a, var, EPS, None, ALU.add))
            dve.wait_ge(bn_sqrt, 1)
            step(nc.vector.reciprocal(t3, root))
            step(nc.vector.tensor_tensor(t3, t3, a, ALU.mult))
            step(nc.vector.tensor_tensor(t3, t3, root, ALU.add))
            step(nc.vector.tensor_scalar(t3, t3, 0.5, None, ALU.mult))
            step(nc.vector.reciprocal(root, t3))
            step(nc.vector.tensor_tensor(bn_scale[:, :, :], root, gamma, ALU.mult))
            step(nc.vector.tensor_tensor(t3, bn_scale[:, :, :], mean, ALU.mult))
            nc.vector.tensor_tensor(bn_shift[:, :, :], beta, t3, ALU.subtract).then_inc(setup_done, 1)

            first = 2 * STEPS - SPLIT_FIRST
            conv1(0, 0, {first + n: [lambda n=n: low_weights(n)] for n in range(SPLIT_FIRST)})
            conv1(0, 1, {n: [lambda n=n: low_weights(SPLIT_FIRST + n)] for n in range(5 * T - SPLIT_FIRST)})
            dve.wait_ge(bias_in, 16 * 4 * RH)
            for half in range(2):
                raw = bias_raw[:, half * J * HEADS:(half + 1) * J * HEADS]
                backwards = bass.AP(raw.tensor, raw.offset + (J - 1) * HEADS, [raw.ap[0], [1, HEADS], [-HEADS, J]])
                last = nc.vector.tensor_copy(bias[:, half, :, :], backwards)
            step(last)

            def iteration(i):
                conv2_, att, conv1_, out0, out1 = works(i)

                if isinstance(i, int) and i == 0:
                    def softmax(p):
                        add_bias(0, p, 0)
                        add_bias(0, p, 1)
                        maximum(0, p)
                        total(0, p)
                        invert(0, p)

                    conv1(1, 0, {})
                    conv1(1, 1, {2 * STEPS - 2: [lambda: softmax(0), lambda: softmax(1)]})
                    return

                def unit(there, convolution, g, u, between):
                    if there:
                        convolution(g, u, between)
                        return
                    for k in sorted(between):
                        for other in between[k]:
                            other()

                unit(conv2_, conv2, i - 1, 0, {})
                between = {}
                if att:
                    between.update({
                        15: [lambda: add_bias(i, 0, 0), lambda: add_bias(i, 0, 1)],
                    })
                unit(conv2_, conv2, i - 1, 1, between)
                between = {}
                if att:
                    between.update({
                        0: [lambda: maximum(i, 0)],
                        5: [lambda: total(i, 0)],
                        6: [lambda: invert(i, 0)],
                        15: [lambda: add_bias(i, 1, 0)],
                    })
                unit(conv1_, conv1, i + 1, 0, between)
                between = {}
                if att:
                    between.update({
                        0: [lambda: add_bias(i, 1, 1), lambda: maximum(i, 1)],
                        2: [lambda: total(i, 1), lambda: invert(i, 1)],
                    })
                if out0:
                    between.update({
                        8: [lambda: add_mlp0(i, 0)],
                        9: [lambda: add_mlp0(i, 1)],
                        14: [lambda: add_mlp0(i, 2)],
                        16: [lambda: add_mlp0(i, 3)],
                    })
                unit(conv1_, conv1, i + 1, 1, between)

            iteration(0)
            iteration(1)
            with dve.Fori(2, GROUPS - 1) as i:
                iteration(i)
            for i in range(GROUPS - 1, GROUPS + 2):
                iteration(i)

        @block.gpsimd
        def _(pool):
            def low1(g, t):
                b = t % 2
                pool.wait_ge(hi1_done, g * T + (t + 1))
                nc.gpsimd.tensor_tensor(by_image(y_lo[:, t, :]), staged(b),
                                        by_image(y_hi[:, t, :].bitcast(F32)),
                                        ALU.subtract).then_inc(lo1_done, 1)

            def bilinear(g, t):
                full = y_stage[:, t % 2, :]

                def rows(odd):
                    return bass.AP(full.tensor, full.offset + odd * G * W,
                                   [full.ap[0], [W, G], [2 * G * W, RH], [1, W]])

                def by_row(w):
                    f = frac[:, w, :]
                    return bass.AP(f.tensor, f.offset, [f.ap[0], [0, G], [1, RH], [0, W]])

                def by_column(w):
                    f = frac[:, w, :]
                    return bass.AP(f.tensor, f.offset, [f.ap[0], [0, G * RH], [1, RH]])

                columns = bil_a[:, :, :, :].rearrange("p b r c -> p (b r) c")
                left = bil_b[:, 0:2, :, :].rearrange("p b r c -> p (b r c)").rearrange("p (r c) -> p r c", c=RH)
                right = bil_b[:, 2:4, :, :].rearrange("p b r c -> p (b r c)").rearrange("p (r c) -> p r c", c=RH)
                n = g * 20 + 5 * t
                need(pool, bil_done, g * T + t)
                nc.gpsimd.tensor_tensor(bil_a[:, :, :, :], rows(0), by_row(0), ALU.mult).then_inc(bil_step, 1)
                nc.gpsimd.tensor_tensor(bil_b[:, :, :, :], rows(1), by_row(1), ALU.mult).then_inc(bil_step, 1)
                pool.wait_ge(bil_step, n + 2)
                nc.gpsimd.tensor_tensor(bil_a[:, :, :, :], bil_a[:, :, :, :], bil_b[:, :, :, :],
                                        ALU.add).then_inc(bil_step, 1)
                pool.wait_ge(bil_step, n + 3)
                nc.gpsimd.tensor_tensor(left, columns[:, :, 0:W:2], by_column(0), ALU.mult).then_inc(bil_step, 1)
                nc.gpsimd.tensor_tensor(right, columns[:, :, 1:W:2], by_column(1), ALU.mult).then_inc(bil_step, 1)
                pool.wait_ge(bil_step, n + 5)
                nc.gpsimd.tensor_tensor(yb[:, t, :, 0:J], left.rearrange("p (b r) c -> p b (r c)", b=G),
                                        right.rearrange("p (b r) c -> p b (r c)", b=G), ALU.add).then_inc(bil_done, 1)

            def low2(g, t):
                pool.wait_ge(hi2_done, g * T + (t + 1))
                nc.gpsimd.tensor_tensor(by_image(o_lo[:, t, :]), staged(t % 2),
                                        by_image(o_hi[:, t, :].bitcast(F32)),
                                        ALU.subtract).then_inc(lo2_done, 1)

            def wide(row):
                return bass.AP(row[:, :].tensor, row[:, :].offset, [row[:, :].ap[0], [1, 16], [0, J]])

            def less_max(i, p):
                pool.wait_ge(max_done, i * 2 + (p + 1))
                nc.gpsimd.tensor_tensor(s_rows, s_rows, wide(row_max), ALU.subtract).then_inc(sub_done, 1)

            def normalise(i, p):
                pool.wait_ge(inv_done, i * 2 + (p + 1))
                nc.gpsimd.tensor_tensor(s_rows, s_rows, wide(row_inv), ALU.mult).then_inc(norm_done, 1)

            def residual(i, p, t):
                g = i - 1 - p
                pool.wait_ge(res_ready[t], (g * 2 + (p + 1)) * 16)
                pool.wait_ge(tile_taken, out_tile(g, p, t) + 1)
                nc.gpsimd.tensor_tensor(res[:, t, :], z_sb[:, t, :], res[:, t, :], ALU.add).then_inc(r_done, 1)

            def lowh(i, p, t):
                g = i - 1 - p
                pool.wait_ge(hih_done, g * 8 + (4 * p + t + 1))
                nc.gpsimd.tensor_tensor(h_lo[:, t, :], z_sb[:, t, :], h_hi[:, t, :].bitcast(F32),
                                        ALU.subtract).then_inc(loh_done, 1)

            def add_mlp1(i, t):
                pool.wait_ge(tile_taken, tile_no(i, "MLP1", t) + 1)
                nc.gpsimd.tensor_tensor(res[:, t, :], z_sb[:, t, :], res[:, t, :], ALU.add).then_inc(added1, 1)

            nc.gpsimd.memset(ident[:, :], 0.0).then_inc(ident_zero, 1)
            pool.wait_ge(ident_zero, 1)
            nc.gpsimd.affine_select(out=ident[:, :], in_=ident[:, :], compare_op=ALU.not_equal, fill=1.0, base=0,
                                    pattern=[[-1, P]], channel_multiplier=1).then_inc(ident_done, 1)
            at = np.linspace(0.0, H - 1, RH, dtype=np.float32)
            for j in range(RH):
                w = float(np.float32(at[j] - np.float32(2 * j)))
                nc.gpsimd.memset(frac[:, 0, j:j + 1], float(np.float32(1.0) - np.float32(w)))
                nc.gpsimd.memset(frac[:, 1, j:j + 1], w)
            nc.gpsimd.memset(yb[:, :, :, :], 0.0)
            nc.gpsimd.memset(s_sb[:, :, :, :], 0.0).then_inc(consts_done, 1)
            pool.wait_ge(consts_done, 1)
            for t in (0, 1):
                low1(0, t)
            for t in (0, 1):
                bilinear(0, t)
            pool.wait_ge(wt_ready, 4 * T)
            nc.gpsimd.memset(o_pad[:, :], 0.0).then_inc(consts_done, 1)

            def iteration(i):
                conv2_, att, conv1_, out0, out1 = works(i)
                if out1:
                    residual(i, 1, 0)
                if att:
                    low1(i, 2)
                    low1(i, 3)
                    bilinear(i, 2)
                    bilinear(i, 3)
                if out1:
                    residual(i, 1, 1)
                    residual(i, 1, 2)
                    lowh(i, 1, 0)
                if conv2_:
                    low2(i - 1, 0)
                if out1:
                    lowh(i, 1, 1)
                    residual(i, 1, 3)
                if conv2_:
                    low2(i - 1, 1)
                if out1:
                    lowh(i, 1, 2)
                    lowh(i, 1, 3)
                if conv2_:
                    low2(i - 1, 2)
                if att:
                    less_max(i, 0)
                if out1:
                    add_mlp1(i, 0)
                    add_mlp1(i, 1)
                if att:
                    normalise(i, 0)
                if conv2_:
                    low2(i - 1, 3)
                if out1:
                    add_mlp1(i, 2)
                    add_mlp1(i, 3)
                if out0:
                    residual(i, 0, 0)
                    residual(i, 0, 1)
                if conv1_:
                    low1(i + 1, 0)
                if out0:
                    lowh(i, 0, 0)
                if att:
                    less_max(i, 1)
                if out0:
                    residual(i, 0, 2)
                    lowh(i, 0, 1)
                    residual(i, 0, 3)
                if att:
                    normalise(i, 1)
                if out0:
                    lowh(i, 0, 2)
                    lowh(i, 0, 3)
                if conv1_:
                    bilinear(i + 1, 0)
                    low1(i + 1, 1)
                    bilinear(i + 1, 1)

            iteration(0)
            iteration(1)
            with pool.Fori(2, GROUPS - 1) as i:
                iteration(i)
            for i in range(GROUPS - 1, GROUPS + 2):
                iteration(i)

        @block.tensor
        def _(pe):
            def product(bank, name, hi, lo, s_ready, t, cols):
                for s in range(T):
                    s_ready(s)
                    sides = [(w_hi, hi), (w_hi, lo), (w_lo, hi)]
                    for m, (w, r) in enumerate(sides):
                        last = nc.tensor.matmul(mm_ps[:, bank, 0:PAIR], w[name][:, s, t, :],
                                                r[:, s, cols:cols + PAIR],
                                                start=(s == 0 and m == 0), stop=(s == T - 1 and m == 2))
                return last

            def bank_free(i, what, t):
                if t >= 2:
                    what, t = what + "+", t - 2
                at = stages(i).index(what)
                if at:
                    last, n = stages(i)[at - 1], i
                else:
                    last, n = (stages(i - 1) or ORDER)[-1], i - 1
                if last.startswith("MLP0") and not (isinstance(n, int) and n < 1):
                    pe.wait_ge(added0, n * T + ((2 if last == "MLP0+" else 0) + t + 1 - T))
                else:
                    need(pe, tile_taken, tile_no(i, what, t) - 1)

            def out_product(g, p, t):
                if p == 0:
                    bank_free(g + 1, "OUT0", t)
                elif t < 2:
                    bank_free(g + 1, "OUT1A", t)
                else:
                    bank_free(g + 2, "OUT1B", t - 2)

                def s_ready(s):
                    if p == 0 and t == 0:
                        pe.wait_ge(lo2_done, g * T + (s + 1))
                product(t % 2, "o", o_hi, o_lo, s_ready, t, PAIR * p).then_inc(tile_ready, 1)

            def mlp(i, p, t):
                g = i - 1 - p
                bank_free(i, f"MLP{p}", t)

                def s_ready(s):
                    if t == 0:
                        pe.wait_ge(loh_done, g * 8 + (4 * p + s + 1))
                product(t % 2, "m", h_hi, h_lo, s_ready, t, 0).then_inc(tile_ready if p else mlp0_ready, 1)

            def queries(i, p, t):
                bank_free(i, f"Q{p}", t)

                def s_ready(s):
                    if p == 0 and t == 0:
                        pe.wait_ge(lo1_done, i * T + (s + 1))
                product(t % 2, "q", y_hi, y_lo, s_ready, t, PAIR * p).then_inc(tile_ready, 1)

            def keys(i, h):
                bank_free(i, "K", h)
                for s in range(T):
                    if h == 0:
                        pe.wait_ge(bil_done, i * T + (s + 1))
                    last = nc.tensor.matmul(mm_ps[:, h % 2, 0:G * J], w_full["k"][:, s, h, :],
                                            yb[:, s, :, 0:J], start=(s == 0), stop=(s == T - 1))
                last.then_inc(tile_ready, 1)

            def values(i, p):
                bank_free(i, "V", p)
                for s in range(T):
                    if p == 0:
                        pe.wait_ge(bil_done, i * T + (s + 1))
                    last = nc.tensor.matmul(mm_ps[:, p, :],
                                            yb[:, s, 2 * p:2 * p + 2, :].rearrange("p b j -> p (b j)"),
                                            w_full["v"][:, s, :, :].rearrange("p t n -> p (t n)"),
                                            start=(s == 0), stop=(s == T - 1))
                last.then_inc(tile_ready, 1)

            def scores(i, p, b):
                pe.wait_ge(tile_taken, tile_no(i, "Q1" if p else "K", 3) + 1)
                need(pe, pt_taken, i * 2 + p)
                for half in range(2):
                    for h in range(HEADS):
                        at = PAIR * p + HW * b + HALF * half
                        to = (half * HEADS + h) * J
                        last = nc.tensor.matmul(att_ps[0:HALF, b, to:to + J], q_sb[:, h, at:at + HALF],
                                                k_sb[:, h, J * (2 * p + b):J * (2 * p + b + 1)],
                                                start=True, stop=True)
                last.then_inc(scores_ready, 1)

            def turn(i, p):
                pe.wait_ge(norm_done, i * 2 + (p + 1))
                for half in range(2):
                    for h in range(HEADS):
                        both = s_sb[:, half * HEADS + h, :, :].rearrange("p b j -> p (b j)")
                        at = HW * (h % 2) + HALF * half
                        last = nc.tensor.transpose(att_ps[:, h // 2, at:at + HALF], both, ident[0:HALF, 0:HALF])
                last.then_inc(pt_ready, 1)

            def attend(i, p, hp):
                pe.wait_ge(pt_taken, i * 2 + (p + 1))
                for b in range(2):
                    bank_free(i, f"PV{p}", 2 * hp + b)
                    for h in (2 * hp, 2 * hp + 1):
                        mm = nc.tensor.matmul(mm_ps[:, b, HW * (h % 2):HW * (h % 2 + 1)],
                                              v_sb[JP * b:JP * b + J, p, DH * h:DH * (h + 1)],
                                              pt_sb[JP * b:JP * b + J, h, :], start=True, stop=True)
                    mm.then_inc(tile_ready, 1)

            pe.wait_ge(ident_done, 1)
            for m in range(5):
                pe.wait_ge(wn_in[m % 2], 16 * (m // 2 + 1))
                for s in range(T):
                    n = 4 * m + s
                    need(pe, wt_hi, n - 1)
                    need(pe, wt_lo, n - 1)
                    for t in range(T):
                        last = nc.tensor.transpose(mm_ps[:, s % 2, P * t:P * (t + 1)], wn[m % 2][:, t, s:C:T],
                                                   ident[:, :])
                    last.then_inc(wt_ready, 1)
            pe.wait_ge(wt_hi, 20)
            pe.wait_ge(wt_lo, 20)

            def iteration(i):
                conv2_, att, conv1_, out0, out1 = works(i)
                if out1:
                    out_product(i - 2, 1, 2)
                    out_product(i - 2, 1, 3)
                if att:
                    queries(i, 0, 0)
                    queries(i, 0, 1)
                    queries(i, 0, 2)
                    queries(i, 0, 3)
                    values(i, 0)
                    values(i, 1)
                    keys(i, 0)
                    keys(i, 1)
                    keys(i, 2)
                    keys(i, 3)
                    queries(i, 1, 0)
                    queries(i, 1, 1)
                    scores(i, 0, 0)
                    scores(i, 0, 1)
                if out1:
                    mlp(i, 1, 0)
                    mlp(i, 1, 1)
                if att:
                    queries(i, 1, 2)
                    queries(i, 1, 3)
                if out1:
                    mlp(i, 1, 2)
                    mlp(i, 1, 3)
                if att:
                    turn(i, 0)
                if out0:
                    out_product(i - 1, 0, 0)
                    out_product(i - 1, 0, 1)
                if att:
                    scores(i, 1, 0)
                    attend(i, 0, 0)
                    scores(i, 1, 1)
                if out0:
                    out_product(i - 1, 0, 2)
                    out_product(i - 1, 0, 3)
                    out_product(i - 1, 1, 0)
                    out_product(i - 1, 1, 1)
                if att:
                    attend(i, 0, 1)
                    turn(i, 1)
                if out0:
                    mlp(i, 0, 0)
                    mlp(i, 0, 1)
                if att:
                    attend(i, 1, 0)
                    attend(i, 1, 1)
                if out0:
                    mlp(i, 0, 2)
                    mlp(i, 0, 3)

            iteration(0)
            iteration(1)
            with pe.Fori(2, GROUPS - 1) as i:
                iteration(i)
            for i in range(GROUPS - 1, GROUPS + 2):
                iteration(i)


_INS = ['x', 'L0_conv_bn1_g', 'L0_conv_bn1_b', 'L0_conv_bn1_m', 'L0_conv_bn1_v', 'L0_conv_w_qkv_dw',
        'L0_conv_w_qkv_pw', 'L0_conv_rel_table', 'L0_conv_w_out_dw', 'L0_conv_w_out_pw', 'L0_conv_bn2_g',
        'L0_conv_bn2_b', 'L0_conv_bn2_m', 'L0_conv_bn2_v', 'L0_conv_w_mlp']
_OUTS = [((B, C, H, W), 'float32')]


def kernel(**inputs):
    import numpy as _np
    import concourse.bacc as _bacc
    from concourse import mybir as _mybir
    from concourse.bass_utils import run_bass_kernel_spmd as _run

    nc = _bacc.Bacc("TRN2", target_bir_lowering=False, num_devices=1)
    arrays, args = {}, []
    for name in _INS:
        a = _np.ascontiguousarray(inputs[name])
        arrays[f"in_{name}_dram"] = a
        args.append(nc.dram_tensor(f"in_{name}_dram", a.shape, _mybir.dt.from_np(a.dtype), kind="ExternalInput").ap())
    for i, (shape, dtype) in enumerate(_OUTS):
        dt = _mybir.dt.from_np(_np.dtype(dtype))
        args.append(nc.dram_tensor(f"out_{i}_dram", shape, dt, kind="ExternalOutput").ap())
    build(nc, *args)
    r = _run(nc, [arrays], core_ids=[0])
    got = tuple(r.results[0][f"out_{i}_dram"] for i in range(len(_OUTS)))
    return got[0]
```
